# Optimizing a Trainium2 kernel written in Bass

```python
import numpy as np
import jax
import jax.numpy as jnp

def _softmax(x, axis=-1):
    return jax.nn.softmax(x, axis=axis)
def _gelu(x):
    return jax.nn.gelu(x, approximate=True)
def _silu(x):
    return jax.nn.silu(x)
def _sigmoid(x):
    return jax.nn.sigmoid(x)
def _layernorm(x, axis=-1, eps=1e-5):
    m = jnp.mean(x, axis=axis, keepdims=True)
    v = jnp.var(x, axis=axis, keepdims=True)
    return (x - m) / jnp.sqrt(v + eps)
def _scatter_add(tgt, idx, src, axis=0):
    return tgt.at[idx].add(src)
def _segment_sum(src, seg, n):
    return jax.ops.segment_sum(src, seg, n)

kernel_name = 'mk_conv_seq_d1_conv_nchw256_5c1ebc'

def setup_inputs(seed: int = 0):
    np.random.seed(seed)
    _w = jnp.asarray
    def _rec_inputs():
        import jax
        import jax.numpy as jnp
        _gk = jax.random.key(seed)
        x = -0.0003929 + 0.9999 * jax.random.normal(jax.random.fold_in(_gk, 1), (16, 256, 64, 64), jnp.float32)
        return x
    x = _rec_inputs()
    def _L0_conv_setup():
        import jax, jax.numpy as jnp
        import numpy as np
        BN_EPS = 1e-05

        def conv1x1(x, w, b):
            return jnp.einsum('bchw,oc->bohw', x, w) + b[None, :, None, None]

        def maxpool2(x):
            b, c, h, w = x.shape
            return x.reshape(b, c, h // 2, 2, w // 2, 2).max(axis=(3, 5))
        key = jax.random.key(seed)
        ks = jax.random.split(key, 11)
        C, IC = (256, 128)
        s = 1.0 / np.sqrt(C)
        si = 1.0 / np.sqrt(IC)
        return {'x': jax.random.normal(ks[0], (16, C, 64, 64), dtype=jnp.float32), 'g_w': jax.random.uniform(ks[1], (IC, C), jnp.float32, -s, s), 'g_b': jax.random.uniform(ks[2], (IC,), jnp.float32, -s, s), 'theta_w': jax.random.uniform(ks[3], (IC, C), jnp.float32, -s, s), 'theta_b': jax.random.uniform(ks[4], (IC,), jnp.float32, -s, s), 'phi_w': jax.random.uniform(ks[5], (IC, C), jnp.float32, -s, s), 'phi_b': jax.random.uniform(ks[6], (IC,), jnp.float32, -s, s), 'W_w': jax.random.uniform(ks[7], (C, IC), jnp.float32, -si, si), 'W_b': jax.random.uniform(ks[8], (C,), jnp.float32, -si, si), 'bn_gamma': jax.random.uniform(ks[9], (C,), jnp.float32, 0.5, 1.5), 'bn_beta': jax.random.uniform(ks[10], (C,), jnp.float32, -0.1, 0.1)}
    _L0_conv_all = _L0_conv_setup()
    _L0_conv_in = {k: v for k, v in _L0_conv_all.items() if k in ('g_w', 'g_b', 'theta_w', 'theta_b', 'phi_w', 'phi_b', 'W_w', 'W_b', 'bn_gamma', 'bn_beta', )}
    del _L0_conv_all

    return {
        "x": x,
        "L0_conv_g_w": _L0_conv_in["g_w"],
        "L0_conv_g_b": _L0_conv_in["g_b"],
        "L0_conv_theta_w": _L0_conv_in["theta_w"],
        "L0_conv_theta_b": _L0_conv_in["theta_b"],
        "L0_conv_phi_w": _L0_conv_in["phi_w"],
        "L0_conv_phi_b": _L0_conv_in["phi_b"],
        "L0_conv_W_w": _L0_conv_in["W_w"],
        "L0_conv_W_b": _L0_conv_in["W_b"],
        "L0_conv_bn_gamma": _L0_conv_in["bn_gamma"],
        "L0_conv_bn_beta": _L0_conv_in["bn_beta"],
    }

def reference(x, L0_conv_g_w, L0_conv_g_b, L0_conv_theta_w, L0_conv_theta_b, L0_conv_phi_w, L0_conv_phi_b, L0_conv_W_w, L0_conv_W_b, L0_conv_bn_gamma, L0_conv_bn_beta):
    import jax
    import jax.numpy as jnp
    def _L0_conv_ref(x, g_w, g_b, theta_w, theta_b, phi_w, phi_b, W_w, W_b, bn_gamma, bn_beta):
        import jax, jax.numpy as jnp
        import numpy as np
        BN_EPS = 1e-05

        def conv1x1(x, w, b):
            return jnp.einsum('bchw,oc->bohw', x, w) + b[None, :, None, None]

        def maxpool2(x):
            b, c, h, w = x.shape
            return x.reshape(b, c, h // 2, 2, w // 2, 2).max(axis=(3, 5))
        b, c, h, w = x.shape
        inter = g_w.shape[0]
        g_x = maxpool2(conv1x1(x, g_w, g_b)).reshape(b, inter, -1).transpose(0, 2, 1)
        theta_x = conv1x1(x, theta_w, theta_b).reshape(b, inter, -1).transpose(0, 2, 1)
        phi_x = maxpool2(conv1x1(x, phi_w, phi_b)).reshape(b, inter, -1)
        f = jnp.einsum('bni,bis->bns', theta_x, phi_x)
        f_div_C = jax.nn.softmax(f, axis=1)
        y = jnp.einsum('bns,bsi->bni', f_div_C, g_x)
        y = y.transpose(0, 2, 1).reshape(b, inter, h, w)
        wy = conv1x1(y, W_w, W_b)
        mean = wy.mean(axis=(0, 2, 3))
        var = ((wy - mean[None, :, None, None]) ** 2).mean(axis=(0, 2, 3))
        wy = (wy - mean[None, :, None, None]) * jax.lax.rsqrt(var + BN_EPS)[None, :, None, None]
        wy = wy * bn_gamma[None, :, None, None] + bn_beta[None, :, None, None]
        return wy + x

    def _gn(v, G=32, eps=1e-5):
        B_, C_, H_, W_ = v.shape
        g = v.reshape(B_, G, C_ // G, H_, W_)
        m = jnp.mean(g, axis=(2, 3, 4), keepdims=True)
        s = jnp.var(g, axis=(2, 3, 4), keepdims=True)
        return ((g - m) / jnp.sqrt(s + eps)).reshape(v.shape)

    def _ln_c(v, eps=1e-6):
        m = jnp.mean(v, axis=1, keepdims=True)
        s = jnp.var(v, axis=1, keepdims=True)
        return (v - m) / jnp.sqrt(s + eps)

    def _ln_t(v, eps=1e-5):
        m = jnp.mean(v, axis=-1, keepdims=True)
        s = jnp.var(v, axis=-1, keepdims=True)
        return (v - m) / jnp.sqrt(s + eps)

    def _to_tokens(v):
        B_, C_, H_, W_ = v.shape
        return v.reshape(B_, C_, H_ * W_).transpose(0, 2, 1)
    def _from_tokens(t, like):
        B_, C_, H_, W_ = like.shape
        return t.transpose(0, 2, 1).reshape(B_, C_, H_, W_)

    x = _L0_conv_ref(x, L0_conv_g_w, L0_conv_g_b, L0_conv_theta_w, L0_conv_theta_b, L0_conv_phi_w, L0_conv_phi_b, L0_conv_W_w, L0_conv_W_b, L0_conv_bn_gamma, L0_conv_bn_beta)
    return x


_drawn_inputs = setup_inputs


def setup_inputs(seed=0):
    import zlib

    import numpy as np

    out = dict(_drawn_inputs(seed))
    spreads = {}
    factors = {}
    for name, (base, spread) in spreads.items():
        noise = np.random.default_rng([zlib.crc32(name.encode()), seed]).standard_normal(out[name].shape)
        drawn = base * np.exp(spread * noise) if base else spread * noise
        out[name] = jnp.asarray(drawn.astype(out[name].dtype))
    for name, factor in factors.items():
        out[name] = (out[name] * factor).astype(out[name].dtype)
    return out
```

```python
from contextlib import ExitStack

import concourse.bass as bass
from concourse import mybir

F32 = mybir.dt.float32
F32R = mybir.dt.float32r
ALU = mybir.AluOpType
ACT = mybir.ActivationFunctionType
AX = mybir.AxisListType

P = 128
NB = 512
BN_EPS = 1e-05

POOL_J = (1, 4, 6)


def nonlocal_block_kernel(nc, x, wT, biases, WT, chan, ident_in, out, y_dram):
    B, C, N = x.shape[0], x.shape[1], x.shape[2]
    CH = C // P
    IC = WT.shape[0]
    K = N // NB
    S = N // 4
    J = S // P
    ROW = 64
    HK = K // 2
    HN = HK * NB
    assert IC == P and C == 2 * P and J == K == 8 and N == K * NB
    NPOOL = len(POOL_J)
    NDVE = J - NPOOL

    x_v = x.rearrange("b (c p) n -> b p c n", p=P)
    out_v = out.rearrange("b (c p) n -> b p c n", p=P)

    ctx = ExitStack()
    with ctx:
        def sb(name, shape, dt=F32):
            return ctx.enter_context(nc.sbuf_tensor(name, shape, dt))

        def ps(name, shape):
            return ctx.enter_context(nc.psum_tensor(name, shape, F32))

        def sem(name):
            return ctx.enter_context(nc.semaphore(name))

        scores = sb("scores", [P, J, N])
        ring_hi = sb("ring_hi", [P, 4, NB], F32R)
        ring_lo = sb("ring_lo", [P, 4, NB], F32R)
        x_raw = sb("x_raw", [P, 2, CH, NB])
        xm_hi = sb("xm_hi", [P, CH, NB], F32R)
        xm_lo = sb("xm_lo", [P, CH, NB], F32R)
        th_hi = sb("th_hi", [P, NB], F32R)
        th_lo = sb("th_lo", [P, NB], F32R)
        phi_hi = sb("phi_hi", [P, S], F32R)
        phi_lo = sb("phi_lo", [P, S], F32R)
        phi_raw = sb("phi_raw", [P, 2, P])
        g_raw = sb("g_raw", [P, 2, P])
        g_bias = sb("g_bias", [P, 2, P])
        gT = sb("gT", [P, 2, J, P])
        gn_hi = sb("gn_hi", [P, J, P], F32R)
        gn_lo = sb("gn_lo", [P, J, P], F32R)
        w_hi = sb("w_hi", [P, CH, 3, P], F32R)
        w_lo = sb("w_lo", [P, CH, 3, P], F32R)
        W_hi = sb("W_hi", [P, C], F32R)
        W_lo = sb("W_lo", [P, C], F32R)
        y32 = sb("y32", [P, NB])
        y_hi = sb("y_hi", [P, NB], F32R)
        y_lo = sb("y_lo", [P, NB], F32R)
        ident = sb("ident", [P, P])
        bias = sb("bias", [P, 3])
        chans = sb("chans", [P, CH, 3])
        block_max = sb("block_max", [P, J, K])
        neg_max = sb("neg_max", [P, 2, J])
        half_sum = sb("half_sum", [P, 2, J])
        neg_all = sb("neg_all", [P, J])
        shift_h = sb("shift_h", [P, 2, J])
        corr = sb("corr", [P, 2, J])
        part_sum = sb("part_sum", [P, 2, J])
        total = sb("total", [P, J])
        inv_total = sb("inv_total", [P, J])
        factor = sb("factor", [P, 2, J])
        bn_blk = sb("bn_blk", [P, CH, K, 6])
        bn_img = sb("bn_img", [P, CH, 2])
        bn_all = sb("bn_all", [P, CH, B, 3])
        tokens = sb("tokens", [P, CH, 1])
        bn_tot = sb("bn_tot", [P, CH, 2])
        bn_tmp = sb("bn_tmp", [P, 8, CH])
        bn_scale = sb("bn_scale", [P, CH])
        bn_shift = sb("bn_shift", [P, CH])

        w_stage = scores[:, 0, 0:CH * 3 * P].rearrange("p (c t i) -> p c t i", c=CH, t=3)
        W_stage = scores[:, 0, 1024:1024 + C]
        QT = 2 * NB
        NQ = N // QT
        x2 = [scores[:, q, 0:CH * QT].rearrange("p (c n) -> p c n", c=CH) for q in range(NQ)]
        y2 = [scores[:, q, CH * QT:CH * QT + QT] for q in range(NQ)]
        o2 = [scores[:, NQ + q, 0:CH * QT].rearrange("p (c n) -> p c n", c=CH) for q in range(NQ)]

        f_ps = ps("f_ps", [P, 4, NB])
        ty_ps = ps("ty_ps", [P, 2, NB])
        t_ps = ty_ps[:, 0, :]
        y_ps = ty_ps[:, 1, :]
        wy_ps = ps("wy_ps", [P, CH, NB])
        pairs = [f_ps[:, 0:2, :], f_ps[:, 2:4, :], ty_ps[:, :, :], wy_ps[:, :, :]]

        w_in = sem("w_in")
        w_split_hi = sem("w_split_hi")
        w_split_lo = sem("w_split_lo")
        x_in = [sem("x_in0"), sem("x_in1")]
        y_out = sem("y_out")
        xhi_proj = sem("xhi_proj")
        xhi_theta = sem("xhi_theta")
        xlo_made = sem("xlo_made")
        phi_mm = sem("phi_mm")
        g_mm = sem("g_mm")
        gT_mm = sem("gT_mm")
        theta_mm = sem("theta_mm")
        f_mm = sem("f_mm")
        y_mm = sem("y_mm")
        wy_mm = sem("wy_mm")
        phi_pooled = sem("phi_pooled")
        g_pooled = sem("g_pooled")
        phi_hi_made = sem("phi_hi_made")
        phi_lo_made = sem("phi_lo_made")
        g_biased = sem("g_biased")
        gT_copied = sem("gT_copied")
        th_hi_made = sem("th_hi_made")
        th_lo_made = sem("th_lo_made")
        f_stored = sem("f_stored")
        max_made = sem("max_made")
        exp_done = sem("exp_done")
        shift_made = sem("shift_made")
        corr_made = sem("corr_made")
        factor_made = sem("factor_made")
        chain = sem("chain")
        gn_hi_made = sem("gn_hi_made")
        gn_lo_made = sem("gn_lo_made")
        p_hi_made = sem("p_hi_made")
        p_lo_dve = sem("p_lo_dve")
        p_lo_pool = sem("p_lo_pool")
        y_copied = sem("y_copied")
        y_hi_made = sem("y_hi_made")
        y_lo_made = sem("y_lo_made")
        bn_done = sem("bn_done")
        bn_img_done = sem("bn_img_done")
        sqrt_done = sem("sqrt_done")
        affine_ready = sem("affine_ready")
        x2_in = [sem(f"x2_in{q}") for q in range(NQ)]
        y2_in = [sem(f"y2_in{q}") for q in range(NQ)]
        out_done = [sem(f"out_done{q}") for q in range(NQ)]
        y2_hi_made = sem("y2_hi_made")
        y2_lo_made = sem("y2_lo_made")
        wy2_mm = sem("wy2_mm")
        wy2_scaled = sem("wy2_scaled")
        x_added = sem("x_added")

        def blk(b, k):
            return b * K + k

        def tile(b, k, j):
            return b * (K * J) + (k * J + j)

        def par(b):
            return b % 2

        def wait(eng, s, value):
            if not isinstance(value, int) or value > 0:
                eng.wait_ge(s, value)

        def wait_p_lo(eng, v, k, j):
            if j in POOL_J:
                wait(eng, p_lo_pool, blk(v, k) * NPOOL + (POOL_J.index(j) + 1))
            else:
                wait(eng, p_lo_dve, blk(v, k) * NDVE + (j - sum(q < j for q in POOL_J) + 1))

        def slot(j):
            return (j + 2) % 4

        def proj_x(k):
            if k % 3 == 0:
                return xm_hi[:, :, :], xm_lo[:, :, :]
            s = 2 * (k % 3 - 1)
            return ring_hi[:, s:s + 2, :], ring_lo[:, s:s + 2, :]

        def wait_proj_x_free(eng, b, k):
            if k >= 3:
                wait(eng, g_mm, blk(b, k - 2))
            elif k == 0:
                wait(eng, theta_mm, blk(b, 0))
            elif not (isinstance(b, int) and b < 2):
                wait(eng, y_mm, tile(b - 1, 0, 0))

        def exp_tile(k, j):
            return scores[:, j, k * NB:(k + 1) * NB]

        def f32(ap):
            return ap.bitcast(F32)

        block = ctx.enter_context(nc.Block())

        @block.sync
        def _(sp):
            sp.dma_start(w_stage, wT.rearrange("(c p) t i -> p c t i", p=P)).then_inc(w_in, 16)
            sp.dma_start(W_stage, WT).then_inc(w_in, 16)
            sp.dma_start(bias[:, :], biases).then_inc(w_in, 16)
            sp.dma_start(chans[:, :, :], chan.rearrange("(c p) t -> p c t", p=P)).then_inc(w_in, 16)
            sp.dma_start(ident[:, :], ident_in).then_inc(w_in, 16)

            def load(b, k, theta):
                wait(sp, xlo_made, b * (2 * K) + (K * theta + k - 1))
                sp.dma_start(x_raw[:, k % 2, :, :],
                             x_v[b, :, :, k * NB:(k + 1) * NB]).then_inc(x_in[k % 2], 16)

            def proj_loads(b):
                for k in range(K):
                    load(b, k + 2, False) if k < K - 2 else load(b, k + 2 - K, True)

            def main_loads(b, v=None, more=True):
                for k in range(K):
                    if k < K - 2:
                        load(b, k + 2, True)
                    elif more:
                        load(b + 1, k + 2 - K, False)
                    if v is not None:
                        store_y(v, k)

            def store_y(v, k):
                wait(sp, y_copied, blk(v, k) + 1)
                sp.dma_start(y_dram[v, :, k * NB:(k + 1) * NB], y32[:, :]).then_inc(y_out, 16)

            load(0, 0, False)
            load(0, 1, False)
            proj_loads(0)
            main_loads(0)
            proj_loads(1)
            with sp.Fori(1, B - 1) as b:
                main_loads(b, b - 1)
                proj_loads(b + 1)
            main_loads(B - 1, B - 2, more=False)
            for k in range(K):
                store_y(B - 1, k)

            def load2(b, q):
                if isinstance(b, int) and b == 0:
                    if q == 0:
                        wait_p_lo(sp, B - 1, K - 1, J - 1)
                        sp.wait_ge(p_lo_pool, B * K * NPOOL)
                        sp.wait_ge(p_lo_dve, B * K * NDVE)
                        sp.wait_ge(y_out, 16 * (B * K))
                else:
                    sp.wait_ge(x_added, b * (2 * NQ) + (2 * q - 2 * NQ + 2))
                cols = slice(q * QT, (q + 1) * QT)
                sp.dma_start(y2[q], y_dram[b, :, cols]).then_inc(y2_in[q], 16)
                sp.dma_start(x2[q], x_v[b, :, :, cols]).then_inc(x2_in[q], 16)

            for q in range(NQ):
                load2(0, q)
            with sp.Fori(1, B) as b:
                for q in range(NQ):
                    load2(b, q)
            for q in range(NQ):
                sp.wait_ge(out_done[q], 16 * B)

        @block.tensor
        def _(pe):
            def split_product(acc, parts, start, stop):
                last = None
                n = len(parts)
                for i, (a_hi, a_lo, m_hi, m_lo) in enumerate(parts):
                    nc.tensor.matmul(acc, a_lo, m_hi, start=start and i == 0, stop=False)
                    nc.tensor.matmul(acc, a_hi, m_lo, start=False, stop=False)
                    last = nc.tensor.matmul(acc, a_hi, m_hi, start=False, stop=stop and i == n - 1)
                return last

            def weights(t, x_hi, x_lo):
                return [(w_hi[:, c, t, :], w_lo[:, c, t, :], x_hi[:, c, :], x_lo[:, c, :]) for c in range(CH)]

            def project(b, k):
                wait(pe, xlo_made, b * (2 * K) + (k + 1))
                bank = 2 * (k % 2)
                if k < 2:
                    wait(pe, f_stored, tile(b, 0, 0) - (2 - 2 * k) if not isinstance(b, int) or b else 0)
                else:
                    wait(pe, phi_pooled, blk(b, k - 1))
                    wait(pe, g_pooled, blk(b, k - 1))
                x_hi, x_lo = proj_x(k)
                split_product(f_ps[:, bank, :], weights(1, x_hi, x_lo), True, True).then_inc(phi_mm, 1)
                split_product(f_ps[:, bank + 1, :], weights(2, x_hi, x_lo), True, True).then_inc(g_mm, 1)

            def transpose_g(b, k):
                wait(pe, g_biased, blk(b, k) + 1)
                if k:
                    wait(pe, gT_copied, blk(b, k))
                else:
                    wait(pe, th_lo_made, blk(b, 0))
                nc.tensor.matmul(t_ps[:, 0:P], g_bias[:, k % 2, :], ident[:, :], start=True, stop=True,
                                 is_transpose=True).then_inc(gT_mm, 1)

            def theta(b, k):
                wait(pe, xlo_made, b * (2 * K) + (K + k + 1))
                if k:
                    wait(pe, th_lo_made, blk(b, k))
                else:
                    wait(pe, gT_copied, blk(b, K))
                split_product(t_ps[:, :], weights(0, xm_hi, xm_lo), True, True).then_inc(theta_mm, 1)

            def score(b, k, j):
                if j == 0:
                    wait(pe, th_lo_made, blk(b, k) + 1)
                if k == 0 and j == 0:
                    wait(pe, phi_lo_made, blk(b, K))
                    wait(pe, phi_pooled, blk(b, K))
                    wait(pe, g_pooled, blk(b, K))
                if k or j >= 4:
                    wait(pe, f_stored, tile(b, k, j) - 3)
                cols = slice(j * P, (j + 1) * P)
                split_product(f_ps[:, j % 4, :], [(phi_hi[:, cols], phi_lo[:, cols], th_hi[:, :], th_lo[:, :])],
                              True, True).then_inc(f_mm, 1)

            def attend(v, k, j):
                if k % HK == 0:
                    wait(pe, gn_lo_made, v * (2 * J) + (k // HK * J + j + 1))
                if j == 0:
                    wait(pe, y_copied, blk(v, k))
                wait_p_lo(pe, v, k, j)
                s = slot(j)
                split_product(y_ps[:, :], [(gn_hi[:, j, :], gn_lo[:, j, :], ring_hi[:, s, :], ring_lo[:, s, :])],
                              j == 0, j == J - 1).then_inc(y_mm, 1)

            def output_conv(v, k):
                wait(pe, y_lo_made, blk(v, k) + 1)
                wait(pe, bn_done, blk(v, k))
                for c in range(CH):
                    cols = slice(c * P, (c + 1) * P)
                    last = split_product(wy_ps[:, c, :], [(W_hi[:, cols], W_lo[:, cols], y_hi[:, :], y_lo[:, :])],
                                         True, True)
                last.then_inc(wy_mm, 1)

            def projections(b, v=None):
                for k in range(K):
                    project(b, k)
                    if k == 0 and v is not None:
                        output_conv(v, K - 1)
                    if k:
                        transpose_g(b, k - 1)
                transpose_g(b, K - 1)
                theta(b, 0)

            def main(b=None, v=None):
                for k in range(K):
                    for s in range(J + 2):
                        if b is not None and s < J:
                            score(b, k, s)
                            if s == 4 and k < K - 1:
                                theta(b, k + 1)
                        if v is not None and s >= 2:
                            attend(v, k, s - 2)
                    if v is not None and k:
                        output_conv(v, k - 1)

            pe.wait_ge(w_split_lo, 2)
            projections(0)
            main(0)
            projections(1)
            with pe.Fori(1, B - 1) as b:
                main(b, b - 1)
                projections(b + 1, b - 1)
            main(B - 1, B - 2)
            output_conv(B - 2, K - 1)
            main(None, B - 1)
            output_conv(B - 1, K - 1)


            def output_conv2(b, q):
                pe.wait_ge(y2_lo_made, b * NQ + (q + 1))
                for c in range(CH):
                    m = 2 * q + c
                    if not (isinstance(b, int) and b == 0 and m < 4):
                        pe.wait_ge(wy2_scaled, b * (2 * NQ) + (m - 3))
                    for h in range(2):
                        cols = slice(c * P, (c + 1) * P)
                        s = 2 * (q % 2) + h
                        last = split_product(pairs[m % 4][:, h, :],
                                             [(W_hi[:, cols], W_lo[:, cols], ring_hi[:, s, :], ring_lo[:, s, :])],
                                             True, True)
                    last.then_inc(wy2_mm, 1)

            pe.wait_ge(bn_done, B * K)
            pe.wait_ge(f_stored, tile(B, 0, 0))
            pe.wait_ge(y_copied, B * K)
            pe.wait_ge(th_lo_made, B * K)
            for q in range(NQ):
                output_conv2(0, q)
            with pe.Fori(1, B) as b:
                for q in range(NQ):
                    output_conv2(b, q)

        @block.scalar
        def _(act):
            def exp_half(b, h, j):
                if j == 0:
                    wait(act, max_made, 2 * b + (h + 1))
                    wait(act, factor_made, b)
                cols = scores[:, j, h * HN:(h + 1) * HN]
                nc.scalar.activation(cols, cols, ACT.Exp, bias=neg_max[:, h, j:j + 1],
                                     accum_out=half_sum[:, h, j:j + 1]).then_inc(exp_done, 1)

            def exp_hi(v, k, j):
                if k == 0 and j == 0:
                    wait(act, exp_done, 2 * J * (v + 1))
                if k == 0 and j < 4:
                    if not (isinstance(v, int) and v == B - 1):
                        wait(act, g_mm, blk(v + 1, K if slot(j) < 2 else K - 2))
                    else:
                        wait(act, y_mm, tile(v, 0, j) - 3)
                else:
                    wait(act, y_mm, tile(v, k, j) - 3)
                nc.scalar.activation(ring_hi[:, slot(j), :], exp_tile(k, j), ACT.Identity).then_inc(p_hi_made, 1)

            def theta_x_hi(b, k):
                wait(act, x_in[k % 2], b * (16 * K) + 16 * (K // 2 + k // 2 + 1))
                if k:
                    wait(act, theta_mm, blk(b, k))
                else:
                    wait(act, g_mm, blk(b, K - 1))
                nc.scalar.activation(xm_hi[:, :, :], x_raw[:, k % 2, :, :], ACT.Identity).then_inc(xhi_theta, 1)

            def theta_hi(b, k):
                wait(act, theta_mm, blk(b, k) + 1)
                wait(act, f_mm, tile(b, k, 0))
                nc.scalar.activation(th_hi[:, :], t_ps, ACT.Identity, bias=bias[:, 0:1]).then_inc(th_hi_made, 1)

            def copy_y(v, k):
                wait(act, y_mm, tile(v, k, J))
                wait(act, y_out, v * (16 * K) + 16 * k)
                wait(act, y_lo_made, blk(v, k))
                nc.scalar.copy(y32[:, :], y_ps).then_inc(y_copied, 1)
                act.wait_ge(y_copied, blk(v, k) + 1)
                wait(act, wy_mm, blk(v, k))
                nc.scalar.activation(y_hi[:, :], y32[:, :], ACT.Identity).then_inc(y_hi_made, 1)

            def scaled_g_hi(v, h, j):
                if j == 0:
                    wait(act, factor_made, v + 1)
                wait(act, y_mm, tile(v, HK - 1, j) + 1 if h else tile(v - 1, K - 1, j) + 1
                     if not (isinstance(v, int) and v == 0) else 0)
                nc.scalar.activation(gn_hi[:, j, :], gT[:, par(v), j, :], ACT.Identity,
                                     scale=factor[:, h, j:j + 1]).then_inc(gn_hi_made, 1)

            def split_weights():
                act.wait_ge(w_in, 16 * 5)
                nc.scalar.activation(w_hi[:, :, :, :], w_stage, ACT.Identity).then_inc(w_split_hi, 1)
                nc.scalar.activation(W_hi[:, :], W_stage, ACT.Identity).then_inc(w_split_hi, 1)

            def softmax_corrections(e):
                wait(act, shift_made, 2 * e + 2)
                nc.scalar.activation(corr[:, :, :], shift_h[:, :, :], ACT.Exp).then_inc(corr_made, 1)

            def projections(b, e=None):
                if e is not None:
                    softmax_corrections(e)
                for k in range(K):
                    wait(act, phi_pooled, blk(b, k) + 1)
                    nc.scalar.activation(phi_hi[:, k * P:(k + 1) * P], phi_raw[:, k % 2, :], ACT.Identity,
                                         bias=bias[:, 1:2]).then_inc(phi_hi_made, 1)
                    wait(act, g_pooled, blk(b, k) + 1)
                    if k >= 2:
                        wait(act, gT_mm, blk(b, k - 1))
                    nc.scalar.activation(g_bias[:, k % 2, :], g_raw[:, k % 2, :], ACT.Identity,
                                         bias=bias[:, 2:3]).then_inc(g_biased, 1)
                    if e is not None:
                        exp_half(e, 1, k)
                theta_x_hi(b, 0)
                theta_hi(b, 0)
                if e is not None:
                    start_attending(e)

            def start_attending(v):
                exp_hi(v, 0, 0)
                exp_hi(v, 0, 1)
                for j in range(J):
                    scaled_g_hi(v, 0, j)

            def main(b=None, v=None):
                for k in range(K):
                    for j in range(J):
                        if v is not None:
                            k2, j2 = (k, j + 2) if j + 2 < J else (k + 1, j + 2 - J)
                            if k2 < K:
                                exp_hi(v, k2, j2)
                            if k == HK - 1 and j:
                                scaled_g_hi(v, 1, j - 1)
                        if b is not None:
                            if j == 1 and k < K - 1:
                                theta_x_hi(b, k + 1)
                            if k >= HK and j in (1, 5):
                                exp_half(b, 0, 2 * (k - HK) + (j == 5))
                    if b is not None and k < K - 1:
                        theta_hi(b, k + 1)
                    if v is not None:
                        if k == HK - 1:
                            scaled_g_hi(v, 1, J - 1)
                        copy_y(v, k)

            split_weights()
            projections(0)
            main(0)
            projections(1, 0)
            with act.Fori(1, B - 1) as b:
                main(b, b - 1)
                projections(b + 1, b)
            main(B - 1, B - 2)
            softmax_corrections(B - 1)
            for j in range(J):
                exp_half(B - 1, 1, j)
            start_attending(B - 1)
            main(None, B - 1)

            act.wait_ge(bn_img_done, 2 * B + 1)
            nc.scalar.activation(bn_tmp[:, 1, :], bn_tmp[:, 0, :], ACT.Sqrt).then_inc(sqrt_done, 1)

            def y2_hi(b, q):
                act.wait_ge(y2_in[q], b * 16 + 16)
                if not (isinstance(b, int) and b == 0 and q < 2):
                    act.wait_ge(wy2_mm, b * (2 * NQ) + (2 * q - 2))
                s = 2 * (q % 2)
                nc.scalar.activation(ring_hi[:, s:s + 2, :], y2[q].rearrange("p (h n) -> p h n", h=2),
                                     ACT.Identity).then_inc(y2_hi_made, 1)

            def scale_shift(b, q):
                for c in range(CH):
                    m = 2 * q + c
                    act.wait_ge(wy2_mm, b * (2 * NQ) + (m + 1))
                    if c == 0 and not (isinstance(b, int) and b == 0):
                        act.wait_ge(out_done[q], b * 16)
                    nc.scalar.activation(o2[q][:, c, :].rearrange("p (h n) -> p h n", h=2), pairs[m % 4],
                                         ACT.Identity, bias=bn_shift[:, c:c + 1],
                                         scale=bn_scale[:, c:c + 1]).then_inc(wy2_scaled, 1)

            def store(b, q):
                act.wait_ge(x_added, b * (2 * NQ) + (2 * q + 2))
                act.dma_start(out_v[b, :, :, q * QT:(q + 1) * QT], o2[q]).then_inc(out_done[q], 16)

            def second(b, first=False, last=False):
                for q in range(NQ):
                    if q < NQ - 1:
                        y2_hi(b, q + 1)
                    elif not last:
                        y2_hi(b + 1, 0)
                    scale_shift(b, q)
                    if q:
                        store(b, q - 1)
                    elif not first:
                        store(b - 1, NQ - 1)

            y2_hi(0, 0)
            act.wait_ge(affine_ready, 1)
            second(0, first=True)
            with act.Fori(1, B - 1) as b:
                second(b)
            second(B - 1, last=True)
            store(B - 1, NQ - 1)

        @block.vector
        def _(dve):
            def low_of_weights():
                dve.wait_ge(w_split_hi, 2)
                nc.vector.tensor_tensor(w_lo[:, :, :, :], w_stage, f32(w_hi[:, :, :, :]),
                                        ALU.subtract).then_inc(w_split_lo, 1)
                nc.vector.tensor_tensor(W_lo[:, :], W_stage, f32(W_hi[:, :]), ALU.subtract).then_inc(w_split_lo, 1)
                nc.vector.memset(tokens[:, :, :], float(N)).then_inc(w_split_lo, 1)
                dve.wait_ge(w_split_lo, 3)

            def proj_x_hi(b, k):
                wait(dve, x_in[k % 2], b * (16 * K) + 16 * (k // 2 + 1))
                wait_proj_x_free(dve, b, k)
                nc.vector.tensor_copy(proj_x(k)[0], x_raw[:, k % 2, :, :]).then_inc(xhi_proj, 1)

            def pool_phi_g(b, k):
                bank = 2 * (k % 2)
                window = "p (h a w t) -> p h w a t"
                sizes = dict(a=2, w=ROW // 2, t=2)
                if k >= 2:
                    wait(dve, phi_lo_made, blk(b, k - 1))
                    wait(dve, g_biased, blk(b, k - 1))
                wait(dve, phi_mm, blk(b, k) + 1)
                nc.vector.tensor_reduce(phi_raw[:, k % 2, :].rearrange("p (h w) -> p h w", w=ROW // 2),
                                        f_ps[:, bank, :].rearrange(window, **sizes), AX.XY,
                                        ALU.max).then_inc(phi_pooled, 1)
                wait(dve, g_mm, blk(b, k) + 1)
                nc.vector.tensor_reduce(g_raw[:, k % 2, :].rearrange("p (h w) -> p h w", w=ROW // 2),
                                        f_ps[:, bank + 1, :].rearrange(window, **sizes), AX.XY,
                                        ALU.max).then_inc(g_pooled, 1)

            def phi_low(b, k):
                wait(dve, phi_hi_made, blk(b, k) + 1)
                wait(dve, phi_pooled, blk(b, k) + 1)
                cols = slice(k * P, (k + 1) * P)
                nc.vector.scalar_tensor_tensor(phi_lo[:, cols], phi_raw[:, k % 2, :], bias[:, 1:2],
                                               f32(phi_hi[:, cols]), ALU.add, ALU.subtract).then_inc(phi_lo_made, 1)

            def copy_gT(b, k):
                wait(dve, gT_mm, blk(b, k) + 1)
                nc.vector.tensor_copy(gT[:, par(b), k, :], t_ps[:, 0:P]).then_inc(gT_copied, 1)

            def theta_lo(b, k):
                wait(dve, th_hi_made, blk(b, k) + 1)
                nc.vector.scalar_tensor_tensor(th_lo[:, :], t_ps, bias[:, 0:1], f32(th_hi[:, :]),
                                               ALU.add, ALU.subtract).then_inc(th_lo_made, 1)

            def store_f(b, k, j, v):
                wait(dve, f_mm, tile(b, k, j) + 1)
                if v is not None:
                    wait_p_lo(dve, v, k, j)
                if j == 0:
                    wait(dve, max_made, 2 * b + k // HK)
                nc.vector.tensor_scalar(exp_tile(k, j), f_ps[:, j % 4, :], 1.0, None, ALU.mult, ALU.max,
                                        accum_out=block_max[:, j, k:k + 1]).then_inc(f_stored, 1)

            def exp_lo(v, k, j):
                if j in POOL_J:
                    return
                wait(dve, p_hi_made, tile(v, k, j) + 1)
                nc.vector.tensor_tensor(ring_lo[:, slot(j), :], exp_tile(k, j), f32(ring_hi[:, slot(j), :]),
                                        ALU.subtract).then_inc(p_lo_dve, 1)

            def half_max(b, h):
                wait(dve, f_stored, tile(b, (h + 1) * HK, 0))
                wait(dve, exp_done, b * (2 * J))
                wait(dve, shift_made, b * 2)
                nc.vector.tensor_reduce(neg_max[:, h, :], block_max[:, :, h * HK:(h + 1) * HK], AX.X, ALU.max,
                                        negate=True).then_inc(max_made, 1)

            def max_shift(b):
                wait(dve, max_made, 2 * b + 2)
                wait(dve, corr_made, b)
                nc.vector.tensor_tensor(neg_all[:, :], neg_max[:, 0, :], neg_max[:, 1, :],
                                        ALU.min).then_inc(shift_made, 1)
                wait(dve, shift_made, 2 * b + 1)
                for h in range(2):
                    last = nc.vector.tensor_tensor(shift_h[:, h, :], neg_all[:, :], neg_max[:, h, :], ALU.subtract)
                last.then_inc(shift_made, 1)

            def softmax_factors(b):
                wait(dve, exp_done, (b + 1) * (2 * J))
                wait(dve, corr_made, b + 1)
                wait(dve, gn_lo_made, b * (2 * J))
                nc.vector.tensor_tensor(part_sum[:, :, :], half_sum[:, :, :], corr[:, :, :],
                                        ALU.mult).then_inc(chain, 1)
                wait(dve, chain, 3 * b + 1)
                nc.vector.tensor_tensor(total[:, :], part_sum[:, 0, :], part_sum[:, 1, :], ALU.add).then_inc(chain, 1)
                wait(dve, chain, 3 * b + 2)
                nc.vector.reciprocal(inv_total[:, :], total[:, :]).then_inc(chain, 1)
                wait(dve, chain, 3 * b + 3)
                for h in range(2):
                    last = nc.vector.tensor_tensor(factor[:, h, :], corr[:, h, :], inv_total[:, :], ALU.mult)
                last.then_inc(factor_made, 1)

            def scaled_g_lo(v, h, j):
                if j == 0:
                    wait(dve, factor_made, v + 1)
                wait(dve, gn_hi_made, v * (2 * J) + (h * J + j + 1))
                nc.vector.scalar_tensor_tensor(gn_lo[:, j, :], gT[:, par(v), j, :], factor[:, h, j:j + 1],
                                               f32(gn_hi[:, j, :]), ALU.mult, ALU.subtract).then_inc(gn_lo_made, 1)

            def y_low(v, k):
                wait(dve, y_hi_made, blk(v, k) + 1)
                nc.vector.tensor_tensor(y_lo[:, :], y32[:, :], f32(y_hi[:, :]),
                                        ALU.subtract).then_inc(y_lo_made, 1)

            def block_stats(v, k):
                wait(dve, wy_mm, blk(v, k) + 1)
                if k == 0:
                    wait(dve, bn_img_done, 2 * v)
                for c in range(CH):
                    last = nc.vector.bn_stats(bn_blk[:, c, k, :], wy_ps[:, c, :])
                last.then_inc(bn_done, 1)

            def image_stats(v):
                wait(dve, bn_done, blk(v, K))
                nc.vector.tensor_scalar(bn_all[:, :, bass.ds(v, 1), 0], tokens[:, :, :], 1.0, None, ALU.mult)
                for c in range(CH):
                    last = nc.vector.bn_aggr(bn_img[:, c, :], bn_blk[:, c, :, :])
                last.then_inc(bn_img_done, 1)
                wait(dve, bn_img_done, 2 * v + 1)
                nc.vector.tensor_copy(bn_all[:, :, bass.ds(v, 1), 1], bn_img[:, :, 0:1])
                nc.vector.tensor_scalar(bn_all[:, :, bass.ds(v, 1), 2], bn_img[:, :, 1:2], float(N), None,
                                        ALU.mult).then_inc(bn_img_done, 1)

            def projections(b, e=None, v=None):
                proj_x_hi(b, 0)
                if e is not None:
                    max_shift(e)
                for k in range(K):
                    if k < K - 1:
                        proj_x_hi(b, k + 1)
                    if k >= 2:
                        copy_gT(b, k - 2)
                    if k >= 1:
                        phi_low(b, k - 1)
                    pool_phi_g(b, k)
                    if v is not None:
                        if k == 0:
                            block_stats(v, K - 2)
                        if k == 2:
                            block_stats(v, K - 1)
                        if k == 3:
                            image_stats(v)
                copy_gT(b, K - 2)
                phi_low(b, K - 1)
                copy_gT(b, K - 1)
                theta_lo(b, 0)
                if e is not None:
                    start_attending(e)

            def start_attending(v):
                softmax_factors(v)
                exp_lo(v, 0, 0)
                for j in range(J):
                    scaled_g_lo(v, 0, j)

            def main(b=None, v=None, former=None):
                for k in range(K):
                    for j in range(J):
                        if v is not None:
                            k2, j2 = (k, j + 1) if j + 1 < J else (k + 1, 0)
                            if k2 < K:
                                exp_lo(v, k2, j2)
                        if b is not None:
                            store_f(b, k, j, v)
                        if v is not None:
                            if j == 1 and k >= 1:
                                y_low(v, k - 1)
                            if j == 3 and k >= 2:
                                block_stats(v, k - 2)
                            if k == HK - 1 and j >= 2:
                                scaled_g_lo(v, 1, j - 2)
                    if b is not None and k < K - 1:
                        theta_lo(b, k + 1)
                    if v is not None and k == HK - 1:
                        scaled_g_lo(v, 1, J - 2)
                        scaled_g_lo(v, 1, J - 1)
                    if b is not None and k % HK == HK - 1:
                        half_max(b, k // HK)
                if v is not None:
                    y_low(v, K - 1)

            low_of_weights()
            projections(0)
            main(0)
            projections(1, 0)
            with dve.Fori(1, B - 1) as b:
                main(b, b - 1)
                projections(b + 1, b, b - 1)
            main(B - 1, B - 2)
            max_shift(B - 1)
            block_stats(B - 2, K - 2)
            block_stats(B - 2, K - 1)
            image_stats(B - 2)
            start_attending(B - 1)
            main(None, B - 1)
            block_stats(B - 1, K - 2)
            block_stats(B - 1, K - 1)
            image_stats(B - 1)

            count = [0]

            def link(instruction):
                count[0] += 1
                instruction.then_inc(chain, 1)
                dve.wait_ge(chain, 3 * B + count[0])

            dve.wait_ge(bn_img_done, 2 * B)
            for c in range(CH):
                link(nc.vector.bn_aggr(bn_tot[:, c, :], bn_all[:, c, :, :]))
            var_eps, root, guess, mean_all, tmp, tmp2 = (bn_tmp[:, i, :] for i in range(6))
            nc.vector.tensor_scalar(var_eps, bn_tot[:, :, 1], BN_EPS, None, ALU.add).then_inc(bn_img_done, 1)
            dve.wait_ge(sqrt_done, 1)
            link(nc.vector.reciprocal(guess, root))
            link(nc.vector.tensor_tensor(tmp, guess, guess, ALU.mult))
            link(nc.vector.tensor_tensor(tmp2, tmp, var_eps, ALU.mult))
            link(nc.vector.tensor_scalar(tmp, tmp2, -0.5, 1.5, ALU.mult, ALU.add))
            link(nc.vector.tensor_tensor(tmp2, guess, tmp, ALU.mult))
            link(nc.vector.tensor_tensor(bn_scale[:, :], tmp2, chans[:, :, 1], ALU.mult))
            link(nc.vector.tensor_tensor(mean_all, bn_tot[:, :, 0], chans[:, :, 0], ALU.add))
            link(nc.vector.tensor_tensor(tmp, chans[:, :, 0], mean_all, ALU.subtract))
            link(nc.vector.tensor_tensor(tmp2, tmp, bn_scale[:, :], ALU.mult))
            nc.vector.tensor_tensor(bn_shift[:, :], tmp2, chans[:, :, 2], ALU.add).then_inc(affine_ready, 1)

            def y2_lo(b, q):
                dve.wait_ge(y2_hi_made, b * NQ + (q + 1))
                s = 2 * (q % 2)
                nc.vector.tensor_tensor(ring_lo[:, s:s + 2, :], y2[q].rearrange("p (h n) -> p h n", h=2),
                                        f32(ring_hi[:, s:s + 2, :]), ALU.subtract).then_inc(y2_lo_made, 1)

            def add_x(b, q):
                dve.wait_ge(x2_in[q], b * 16 + 16)
                for c in range(CH):
                    dve.wait_ge(wy2_scaled, b * (2 * NQ) + (2 * q + c + 1))
                    nc.vector.tensor_tensor(o2[q][:, c, :], o2[q][:, c, :], x2[q][:, c, :],
                                            ALU.add).then_inc(x_added, 1)

            def second(b, last):
                for q in range(NQ):
                    if q < NQ - 1:
                        y2_lo(b, q + 1)
                    elif not last:
                        y2_lo(b + 1, 0)
                    add_x(b, q)

            y2_lo(0, 0)
            second(0, False)
            with dve.Fori(1, B - 1) as b:
                second(b, False)
            second(B - 1, True)

        @block.gpsimd
        def _(pool):
            def x_lo(b, k, theta):
                if theta:
                    wait(pool, xhi_theta, blk(b, k) + 1)
                    hi, lo = xm_hi[:, :, :], xm_lo[:, :, :]
                else:
                    wait(pool, xhi_proj, blk(b, k) + 1)
                    hi, lo = proj_x(k)
                nc.gpsimd.tensor_tensor(lo, x_raw[:, k % 2, :, :], f32(hi), ALU.subtract).then_inc(xlo_made, 1)

            def projections(b):
                for k in range(K):
                    x_lo(b, k, False)
                x_lo(b, 0, True)

            def main(b=None, v=None):
                for k in range(K):
                    for n, j in enumerate(POOL_J):
                        if n == 1 and b is not None and k < K - 1:
                            x_lo(b, k + 1, True)
                        if v is not None:
                            wait(pool, p_hi_made, tile(v, k, j) + 1)
                            nc.gpsimd.tensor_tensor(ring_lo[:, slot(j), :], exp_tile(k, j),
                                                    f32(ring_hi[:, slot(j), :]),
                                                    ALU.subtract).then_inc(p_lo_pool, 1)

            projections(0)
            main(0)
            projections(1)
            with pool.Fori(1, B - 1) as b:
                main(b, b - 1)
                projections(b + 1)
            main(B - 1, B - 2)
            main(None, B - 1)


def kernel(**inputs):
    import numpy as np
    import concourse.bacc as bacc
    from concourse import mybir as mb
    from concourse.bass_utils import run_bass_kernel_spmd as run

    def arr(name):
        return np.asarray(inputs[name])

    x = np.ascontiguousarray(arr("x"))
    B, C, H, W = x.shape
    arrays = {
        "x_dram": x.reshape(B, C, H * W),
        "wT_dram": np.ascontiguousarray(np.stack([arr(f"L0_conv_{n}_w").T for n in ("theta", "phi", "g")], axis=1)),
        "bias_dram": np.ascontiguousarray(np.stack([arr(f"L0_conv_{n}_b") for n in ("theta", "phi", "g")], axis=1)),
        "WT_dram": np.ascontiguousarray(arr("L0_conv_W_w").T),
        "chan_dram": np.ascontiguousarray(
            np.stack([arr(f"L0_conv_{n}") for n in ("W_b", "bn_gamma", "bn_beta")], axis=1)),
        "ident_dram": np.eye(128, dtype=np.float32),
    }
    IC = arrays["WT_dram"].shape[0]
    nc = bacc.Bacc("TRN2", target_bir_lowering=False, num_devices=1)
    args = [nc.dram_tensor(n, a.shape, mb.dt.from_np(a.dtype), kind="ExternalInput").ap() for n, a in arrays.items()]
    out = nc.dram_tensor("out_dram", (B, C, H * W), mb.dt.float32, kind="ExternalOutput").ap()
    y = nc.dram_tensor("y_dram", (B, IC, H * W), mb.dt.float32).ap()
    nonlocal_block_kernel(nc, *args, out, y)
    r = run(nc, [arrays], core_ids=[0])
    return r.results[0]["out_dram"].reshape(B, C, H, W)
```

```python
from contextlib import ExitStack

import concourse.bass as bass
from concourse import mybir

F32 = mybir.dt.float32
F32R = mybir.dt.float32r
ALU = mybir.AluOpType
ACT = mybir.ActivationFunctionType
AX = mybir.AxisListType

P = 128
NB = 512
BN_EPS = 1e-05

POOL_J = (1, 3, 5, 7)
DVE_X = (0, 1)


def nonlocal_block_kernel(nc, x, wT, biases, g_bias_rows, WT, chan, ident_in, out, y_dram):
    B, C, N = x.shape[0], x.shape[1], x.shape[2]
    CH = C // P
    IC = WT.shape[0]
    K = N // NB
    S = N // 4
    J = S // P
    ROW = 64
    HK = K // 2
    HN = HK * NB
    assert IC == P and C == 2 * P and J == K == 8 and N == K * NB
    NPOOL = len(POOL_J)
    NDVE = J - NPOOL

    x_v = x.rearrange("b (c p) n -> b p c n", p=P)
    out_v = out.rearrange("b (c p) n -> b p c n", p=P)

    ctx = ExitStack()
    with ctx:
        def sb(name, shape, dt=F32):
            return ctx.enter_context(nc.sbuf_tensor(name, shape, dt))

        def ps(name, shape):
            return ctx.enter_context(nc.psum_tensor(name, shape, F32))

        def sem(name):
            return ctx.enter_context(nc.semaphore(name))

        scores = sb("scores", [P, J, N])
        ring_hi = sb("ring_hi", [P, 4, NB], F32R)
        ring_lo = sb("ring_lo", [P, 4, NB], F32R)
        x_raw = sb("x_raw", [P, 3, CH, NB])
        xm_hi = sb("xm_hi", [P, NB], F32R)
        xm_lo = sb("xm_lo", [P, NB], F32R)
        th_hi = sb("th_hi", [P, NB], F32R)
        th_lo = sb("th_lo", [P, NB], F32R)
        phi_hi = sb("phi_hi", [P, S], F32R)
        phi_lo = sb("phi_lo", [P, S], F32R)
        phi_raw = sb("phi_raw", [P, 2, P])
        g_raw = sb("g_raw", [P, 2, P])
        g_bias = sb("g_bias", [P, P])
        gT = sb("gT", [P, 2, J, P])
        gn_hi = sb("gn_hi", [P, J, P], F32R)
        gn_lo = sb("gn_lo", [P, J, P], F32R)
        w_hi = sb("w_hi", [P, CH, 3, P], F32R)
        w_lo = sb("w_lo", [P, CH, 3, P], F32R)
        W_hi = sb("W_hi", [P, C], F32R)
        W_lo = sb("W_lo", [P, C], F32R)
        y32 = sb("y32", [P, NB])
        y_hi = sb("y_hi", [P, NB], F32R)
        y_lo = sb("y_lo", [P, NB], F32R)
        ident = sb("ident", [P, P])
        bias = sb("bias", [P, 2])
        chans = sb("chans", [P, CH, 3])
        block_max = sb("block_max", [P, J, K])
        neg_max = sb("neg_max", [P, 2, J])
        half_sum = sb("half_sum", [P, 2, J])
        neg_all = sb("neg_all", [P, J])
        shift_h = sb("shift_h", [P, 2, J])
        corr = sb("corr", [P, 2, J])
        part_sum = sb("part_sum", [P, 2, J])
        total = sb("total", [P, J])
        inv_total = sb("inv_total", [P, J])
        factor = sb("factor", [P, 2, J])
        bn_blk = sb("bn_blk", [P, CH, K, 6])
        bn_img = sb("bn_img", [P, CH, 2])
        bn_all = sb("bn_all", [P, CH, B, 3])
        tokens = sb("tokens", [P, CH, 1])
        bn_tot = sb("bn_tot", [P, CH, 2])
        bn_tmp = sb("bn_tmp", [P, 8, CH])
        bn_scale = sb("bn_scale", [P, CH])
        bn_shift = sb("bn_shift", [P, CH])

        w_stage = scores[:, 0, 0:CH * 3 * P].rearrange("p (c t i) -> p c t i", c=CH, t=3)
        W_stage = scores[:, 0, 1024:1024 + C]
        QT = 2 * NB
        NQ = N // QT
        NBUF = K
        IMGS = NBUF // NQ
        ROUNDS = B // IMGS
        assert B % IMGS == 0 and CH * 2 + 2 <= J
        x2 = [[scores[:, 2 * c:2 * c + 2, n * NB:(n + 1) * NB] for c in range(CH)] for n in range(NBUF)]
        y2 = [scores[:, 2 * CH:2 * CH + 2, n * NB:(n + 1) * NB] for n in range(NBUF)]

        f_ps = ps("f_ps", [P, 4, NB])
        ty_ps = ps("ty_ps", [P, 2, NB])
        t_ps = ty_ps[:, 0, :]
        y_ps = ty_ps[:, 1, :]
        wy_ps = ps("wy_ps", [P, CH, NB])
        pairs = [f_ps[:, 0:2, :], f_ps[:, 2:4, :], ty_ps[:, :, :], wy_ps[:, :, :]]

        w_in = sem("w_in")
        ident_arrived = sem("ident_arrived")
        W_arrived = sem("W_arrived")
        w_split_hi = sem("w_split_hi")
        w_split_lo = sem("w_split_lo")
        x_in = [sem(f"x_in{i}") for i in range(3)]
        y_out = sem("y_out")
        xhi_proj = sem("xhi_proj")
        xhi_theta = sem("xhi_theta")
        xlo_proj = sem("xlo_proj")
        xlo_proj_dve = sem("xlo_proj_dve")
        xlo_theta = sem("xlo_theta")
        theta_half_mm = sem("theta_half_mm")
        phi_mm = sem("phi_mm")
        g_mm = sem("g_mm")
        gT_mm = sem("gT_mm")
        theta_mm = sem("theta_mm")
        f_mm = sem("f_mm")
        y_mm = sem("y_mm")
        wy_mm = sem("wy_mm")
        phi_pooled = sem("phi_pooled")
        g_pooled = sem("g_pooled")
        phi_hi_made = sem("phi_hi_made")
        phi_lo_made = sem("phi_lo_made")
        gT_copied = sem("gT_copied")
        th_hi_made = sem("th_hi_made")
        th_lo_made = sem("th_lo_made")
        f_stored = sem("f_stored")
        max_made = sem("max_made")
        exp_done = sem("exp_done")
        shift_made = sem("shift_made")
        corr_made = sem("corr_made")
        factor_made = sem("factor_made")
        chain = sem("chain")
        gn_hi_made = sem("gn_hi_made")
        gn_lo_made = sem("gn_lo_made")
        p_hi_made = sem("p_hi_made")
        p_lo_dve = sem("p_lo_dve")
        p_lo_pool = sem("p_lo_pool")
        y_copied = sem("y_copied")
        y_hi_made = sem("y_hi_made")
        y_lo_made = sem("y_lo_made")
        bn_done = sem("bn_done")
        bn_img_done = sem("bn_img_done")
        sqrt_done = sem("sqrt_done")
        affine_ready = sem("affine_ready")
        x2_in = [sem(f"x2_in{n}") for n in range(NBUF)]
        y2_in = [sem(f"y2_in{n}") for n in range(NBUF)]
        out_done = [sem(f"out_done{n}") for n in range(NBUF)]
        y2_hi_made = sem("y2_hi_made")
        y2_lo_made = sem("y2_lo_made")
        wy2_mm = sem("wy2_mm")
        wy2_scaled = sem("wy2_scaled")
        x_added = sem("x_added")

        def blk(b, k):
            return b * K + k

        def tile(b, k, j):
            return b * (K * J) + (k * J + j)

        def par(b):
            return b % 2

        def wait(eng, s, value):
            if not isinstance(value, int) or value > 0:
                eng.wait_ge(s, value)

        def wait_p_lo(eng, v, k, j):
            if j in POOL_J:
                wait(eng, p_lo_pool, blk(v, k) * NPOOL + (POOL_J.index(j) + 1))
            else:
                wait(eng, p_lo_dve, blk(v, k) * NDVE + (j - sum(q < j for q in POOL_J) + 1))

        def slot(j):
            return j % 4

        ORDER = (0, K - 1) + tuple(range(1, K - 1))

        LOADS = K + K - 2
        BUF = [(i + 1) % 3 if i < K else (i - K) % 3 for i in range(LOADS)]

        def former_load(i):
            former = [q for q in range(i) if BUF[q] == BUF[i]]
            return former[-1] if former else None

        HALVED = [former_load(i) in DVE_X for i in range(LOADS)]

        def arrivals(u, n):
            return sum(32 if HALVED[q] else 16 for q in range(n) if BUF[q] == u)

        def wait_x_in(eng, b, i):
            u = BUF[i]
            eng.wait_ge(x_in[u], b * arrivals(u, LOADS) + arrivals(u, i + 1))

        def wait_x_lo(eng, b, i):
            if i < K:
                eng.wait_ge(xlo_proj, blk(b, i) + 1)
                if i in DVE_X:
                    eng.wait_ge(xlo_proj_dve, b * len(DVE_X) + (DVE_X.index(i) + 1))
            else:
                eng.wait_ge(xlo_theta, b * (2 * (K - 2)) + 2 * (i - K + 1))

        PLACE = (0, 1, "G", 0, 1, "G", 0, 1)

        def proj_x(k):
            if PLACE[k] == "G":
                return tuple(t[:, :, :].rearrange("p (c a) i -> p c (a i)", c=CH) for t in (gn_hi, gn_lo))
            s = 2 * PLACE[k]
            return ring_hi[:, s:s + 2, :], ring_lo[:, s:s + 2, :]

        def wait_proj_x_free(eng, b, k):
            former = [q for q in range(k) if PLACE[q] == PLACE[k]]
            if former:
                wait(eng, g_mm, blk(b, former[-1] + 1))
                if former[-1] == 0:
                    wait(eng, theta_mm, blk(b, 0) + 1)
            elif not (isinstance(b, int) and b < 2):
                wait(eng, y_mm, tile(b - 1, 0, 0) - (2 if PLACE[k] == 0 else 0))
            elif b == 1:
                wait(eng, f_mm, tile(1, 0, 0))

        def exp_tile(k, j):
            return scores[:, j, k * NB:(k + 1) * NB]

        def first_image(b):
            return isinstance(b, int) and b == 0

        def last_image(v):
            return isinstance(v, int) and v == B - 1

        def theta_tile(b, k):
            if first_image(b) and k % 2:
                return ring_hi[:, 3, :], ring_lo[:, 3, :]
            return th_hi[:, :], th_lo[:, :]

        def y_bank(v, k):
            return t_ps if last_image(v) and k % 2 else y_ps

        def f32(ap):
            return ap.bitcast(F32)

        block = ctx.enter_context(nc.Block())

        @block.sync
        def _(sp):
            sp.dma_start(w_stage, wT.rearrange("(c p) t i -> p c t i", p=P)).then_inc(w_in, 16)
            sp.dma_start(bias[:, :], biases).then_inc(w_in, 16)
            sp.dma_start(g_bias[:, :], g_bias_rows).then_inc(w_in, 16)

            def load(b, i):
                k = i if i < K else ORDER[i - K + 2]
                cols = slice(k * NB, (k + 1) * NB)
                former = former_load(i)
                if HALVED[i]:
                    sp.wait_ge(xlo_proj, blk(b, former) + 1)
                    sp.dma_start(x_raw[:, BUF[i], 0, :], x_v[b, :, 0, cols]).then_inc(x_in[BUF[i]], 16)
                    sp.wait_ge(xlo_proj_dve, b * len(DVE_X) + (DVE_X.index(former) + 1))
                    sp.dma_start(x_raw[:, BUF[i], 1, :], x_v[b, :, 1, cols]).then_inc(x_in[BUF[i]], 16)
                    return
                if former is not None:
                    wait_x_lo(sp, b, former)
                elif not (isinstance(b, int) and b == 0):
                    wait_x_lo(sp, b - 1, max(q for q in range(LOADS) if BUF[q] == BUF[i]))
                sp.dma_start(x_raw[:, BUF[i], :, :], x_v[b, :, :, cols]).then_inc(x_in[BUF[i]], 16)

            load(0, 0)
            sp.dma_start(ident[:, :], ident_in).then_inc(ident_arrived, 16)
            load(0, 1)
            sp.dma_start(W_stage, WT).then_inc(W_arrived, 16)
            sp.dma_start(chans[:, :, :], chan.rearrange("(c p) t -> p c t", p=P)).then_inc(W_arrived, 16)
            for i in range(2, LOADS):
                load(0, i)
            with sp.Fori(1, B) as b:
                for i in range(LOADS):
                    load(b, i)

            def load2(t, n):
                if isinstance(t, int) and t == 0:
                    sp.wait_ge(p_lo_pool, (blk(B - 1, n) + 1) * NPOOL)
                    sp.wait_ge(p_lo_dve, (blk(B - 1, n) + 1) * NDVE)
                else:
                    sp.wait_ge(out_done[n], t * (16 * CH))
                b = t * IMGS + n // NQ
                q = n % NQ
                cols = slice(q * QT, (q + 1) * QT)
                sp.dma_start(y2[n], y_dram[b, :, cols].rearrange("p (h n) -> p h n", h=2)).then_inc(y2_in[n], 16)
                for c in range(CH):
                    sp.dma_start(x2[n][c], x_v[b, :, c, cols].rearrange("p (h n) -> p h n", h=2)).then_inc(x2_in[n], 16)

            sp.wait_ge(y_out, 16 * (IMGS * K))
            for n in range(NBUF):
                load2(0, n)
            sp.wait_ge(y_out, 16 * (B * K))
            with sp.Fori(1, ROUNDS) as t:
                for n in range(NBUF):
                    load2(t, n)
            for n in range(NBUF):
                sp.wait_ge(out_done[n], ROUNDS * (16 * CH))

        @block.tensor
        def _(pe):
            def split_product(acc, parts, start, stop):
                last = None
                n = len(parts)
                for i, (a_hi, a_lo, m_hi, m_lo) in enumerate(parts):
                    nc.tensor.matmul(acc, a_lo, m_hi, start=start and i == 0, stop=False)
                    nc.tensor.matmul(acc, a_hi, m_lo, start=False, stop=False)
                    last = nc.tensor.matmul(acc, a_hi, m_hi, start=False, stop=stop and i == n - 1)
                return last

            def weights(t, x_hi, x_lo):
                return [(w_hi[:, c, t, :], w_lo[:, c, t, :], x_hi[:, c, :], x_lo[:, c, :]) for c in range(CH)]

            def project(b, k):
                wait_x_lo(pe, b, k)
                bank = 2 * (k % 2)
                if k < 2:
                    wait(pe, f_stored, tile(b, 0, 0) - (2 - 2 * k) if not isinstance(b, int) or b else 0)
                else:
                    wait(pe, phi_pooled, blk(b, k - 1))
                    wait(pe, g_pooled, blk(b, k - 1))
                x_hi, x_lo = proj_x(k)
                split_product(f_ps[:, bank, :], weights(1, x_hi, x_lo), True, True).then_inc(phi_mm, 1)
                split_product(f_ps[:, bank + 1, :], weights(2, x_hi, x_lo), True, True).then_inc(g_mm, 1)

            def transpose_g(b, k):
                wait(pe, g_pooled, blk(b, k) + 1)
                if k:
                    wait(pe, gT_copied, blk(b, k))
                elif not (isinstance(b, int) and b < 2):
                    wait(pe, y_copied, blk(b - 1, 0))
                nc.tensor.matmul(y_ps[:, 0:P], g_raw[:, k % 2, :], ident[:, :], start=True, stop=True,
                                 is_transpose=True).then_inc(gT_mm, 1)

            def theta_early(b, k):
                wait(pe, th_lo_made, blk(b, k))
                x_hi, x_lo = proj_x(ORDER[k])
                split_product(t_ps, weights(0, x_hi, x_lo), True, True).then_inc(theta_mm, 1)

            def theta_half(b, k, c):
                wait(pe, xlo_theta, b * (2 * (K - 2)) + (2 * (k - 2) + c + 1))
                if c == 0:
                    wait(pe, th_lo_made, blk(b, k))
                split_product(t_ps, [(w_hi[:, c, 0, :], w_lo[:, c, 0, :], xm_hi[:, :], xm_lo[:, :])],
                              c == 0, c == CH - 1).then_inc(theta_mm if c == CH - 1 else theta_half_mm, 1)

            def score(b, k, j):
                if j == 0:
                    wait(pe, th_lo_made, blk(b, k) + 1)
                if k == 0:
                    wait(pe, phi_lo_made, blk(b, j) + 1)
                    if j in (0, 2):
                        wait(pe, g_pooled, blk(b, K - 1 + j // 2))
                if k or j >= 4:
                    wait(pe, f_stored, tile(b, k, j) - 3)
                cols = slice(j * P, (j + 1) * P)
                split_product(f_ps[:, j % 4, :], [(phi_hi[:, cols], phi_lo[:, cols], *theta_tile(b, k))],
                              True, True).then_inc(f_mm, 1)

            def attend(v, k, j):
                if k % HK == 0:
                    wait(pe, gn_lo_made, v * (2 * J) + (k // HK * J + j + 1))
                if j == 0:
                    wait(pe, y_copied, blk(v, max(k - 1, 0)) if last_image(v) else blk(v, k))
                    if last_image(v) and k == 1:
                        wait(pe, th_lo_made, B * K)
                    if k == 0 and not (isinstance(v, int) and v == B - 1):
                        wait(pe, gT_copied, blk(v + 2, 0))
                wait_p_lo(pe, v, k, j)
                s = slot(j)
                split_product(y_bank(v, k), [(gn_hi[:, j, :], gn_lo[:, j, :], ring_hi[:, s, :], ring_lo[:, s, :])],
                              j == 0, j == J - 1).then_inc(y_mm, 1)

            def output_conv(v, k):
                wait(pe, y_lo_made, blk(v, k) + 1)
                wait(pe, bn_done, blk(v, k))
                for c in range(CH):
                    cols = slice(c * P, (c + 1) * P)
                    last = split_product(wy_ps[:, c, :], [(W_hi[:, cols], W_lo[:, cols], y_hi[:, :], y_lo[:, :])],
                                         True, True)
                last.then_inc(wy_mm, 1)

            def projections(b, v=None):
                for k in range(K):
                    project(b, k)
                    if k == 0 and v is not None:
                        output_conv(v, K - 1)
                    if k in ORDER[:2]:
                        theta_early(b, ORDER.index(k))
                    if k:
                        transpose_g(b, k - 1)
                score(b, 0, 0)
                score(b, 0, 1)
                transpose_g(b, K - 1)

            def main(b=None, v=None):
                for k in range(K):
                    for s in range(J + 2):
                        if b is not None and s < J:
                            if k or s >= 2:
                                score(b, k, s)
                            if s == (2 if v is None else 4) and 1 <= k < K - 1:
                                theta_half(b, k + 1, 0)
                        if v is not None:
                            if k == 0 and s == 3:
                                attend(v, k, 0)
                                attend(v, k, 1)
                            elif s >= (4 if k == 0 else 2):
                                attend(v, k, s - 2)
                            if last_image(v) and k and s == J - 2:
                                output_conv(v, k - 1)
                        if b is not None and s == (5 if v is None else J) and 1 <= k < K - 1:
                            theta_half(b, k + 1, 1)
                    if v is not None and k and not last_image(v):
                        output_conv(v, k - 1)

            pe.wait_ge(w_split_lo, 1)
            pe.wait_ge(ident_arrived, 16)
            projections(0)
            main(0)
            projections(1)
            main(1, 0)
            projections(2, 0)
            with pe.Fori(2, B - 1) as b:
                main(b, b - 1)
                projections(b + 1, b - 1)
            main(B - 1, B - 2)
            output_conv(B - 2, K - 1)
            main(None, B - 1)
            output_conv(B - 1, K - 1)


            def output_conv2(t, n):
                pe.wait_ge(y2_lo_made, t * NBUF + (n + 1))
                for c in range(CH):
                    m = CH * n + c
                    if not (isinstance(t, int) and t == 0 and m < 4):
                        pe.wait_ge(x_added, t * (CH * NBUF) + (m - 3))
                    for h in range(2):
                        cols = slice(c * P, (c + 1) * P)
                        s = 2 * (n % 2) + h
                        last = split_product(pairs[m % 4][:, h, :],
                                             [(W_hi[:, cols], W_lo[:, cols], ring_hi[:, s, :], ring_lo[:, s, :])],
                                             True, True)
                    last.then_inc(wy2_mm, 1)

            pe.wait_ge(bn_done, B * K)
            pe.wait_ge(f_stored, tile(B, 0, 0))
            pe.wait_ge(y_copied, B * K)
            pe.wait_ge(th_lo_made, B * K)
            for n in range(NBUF):
                output_conv2(0, n)
            with pe.Fori(1, ROUNDS) as t:
                for n in range(NBUF):
                    output_conv2(t, n)

        @block.scalar
        def _(act):
            def exp_half(b, h, j):
                if j == 0:
                    wait(act, max_made, 2 * b + (h + 1))
                    wait(act, factor_made, b)
                cols = scores[:, j, h * HN:(h + 1) * HN]
                nc.scalar.activation(cols, cols, ACT.Exp, bias=neg_max[:, h, j:j + 1],
                                     accum_out=half_sum[:, h, j:j + 1]).then_inc(exp_done, 1)

            def exp_hi(v, k, j):
                if k % HK == 0 and j == 0:
                    wait(act, exp_done, v * (2 * J) + (J if k == 0 else 2 * J))
                if k == 0 and j < 4:
                    if not (isinstance(v, int) and v == B - 1):
                        if slot(j) < 2:
                            wait(act, g_mm, blk(v + 1, K - 1))
                        else:
                            wait(act, theta_mm, blk(v + 1, 2))
                    else:
                        wait(act, y_mm, tile(v, 0, j) - 3)
                else:
                    wait(act, y_mm, tile(v, k, j) - 3)
                nc.scalar.activation(ring_hi[:, slot(j), :], exp_tile(k, j), ACT.Identity).then_inc(p_hi_made, 1)

            def theta_x_hi(b, k, c):
                i = K + k - 2
                if c == 0:
                    wait_x_in(act, b, i)
                    wait(act, theta_mm, blk(b, k))
                else:
                    wait(act, theta_half_mm, b * (K - 2) + (k - 1))
                nc.scalar.activation(xm_hi[:, :], x_raw[:, BUF[i], c, :], ACT.Identity).then_inc(xhi_theta, 1)

            def theta_hi(b, k):
                wait(act, theta_mm, blk(b, k) + 1)
                wait(act, f_mm, tile(b, max(k - 1, 0) if first_image(b) else k, 0))
                nc.scalar.activation(theta_tile(b, k)[0], t_ps, ACT.Identity, bias=bias[:, 0:1]).then_inc(th_hi_made, 1)

            def copy_y(v, k):
                wait(act, y_mm, tile(v, k, J))
                wait(act, y_out, v * (16 * K) + 16 * k)
                wait(act, y_lo_made, blk(v, k))
                nc.scalar.copy(y32[:, :], y_bank(v, k)).then_inc(y_copied, 1)
                act.wait_ge(y_copied, blk(v, k) + 1)
                wait(act, wy_mm, blk(v, k))
                nc.scalar.activation(y_hi[:, :], y32[:, :], ACT.Identity).then_inc(y_hi_made, 1)
                act.dma_start(y_dram[v, :, ORDER[k] * NB:(ORDER[k] + 1) * NB], y32[:, :]).then_inc(y_out, 16)

            def scaled_g_hi(v, h, j):
                if j == 0:
                    wait(act, factor_made, v + 1)
                    if h == 0 and not (isinstance(v, int) and v == B - 1):
                        wait(act, g_mm, blk(v + 1, 2 + max(q for q in range(K) if PLACE[q] == "G")) - 1)
                wait(act, y_mm, tile(v, HK - 1, j) + 1 if h else tile(v - 1, K - 1, j) + 1
                     if not (isinstance(v, int) and v == 0) else 0)
                nc.scalar.activation(gn_hi[:, j, :], gT[:, par(v), j, :], ACT.Identity,
                                     scale=factor[:, h, j:j + 1]).then_inc(gn_hi_made, 1)

            def split_weights():
                act.wait_ge(w_in, 16 * 3)
                nc.scalar.activation(w_hi[:, :, :, :], w_stage, ACT.Identity).then_inc(w_split_hi, 1)
                act.wait_ge(W_arrived, 16 * 2)
                nc.scalar.activation(W_hi[:, :], W_stage, ACT.Identity).then_inc(w_split_hi, 1)

            def softmax_corrections(e):
                wait(act, shift_made, 2 * e + 2)
                nc.scalar.activation(corr[:, :, :], shift_h[:, :, :], ACT.Exp).then_inc(corr_made, 1)

            def projections(b, e=None):
                if e is not None:
                    exp_half(e, 1, 0)
                    exp_half(e, 1, 1)
                    softmax_corrections(e)
                for k in range(K):
                    if e is not None and k == K - 1:
                        for j in range(6):
                            scaled_g_hi(e, 0, j)
                    wait(act, phi_pooled, blk(b, k) + 1)
                    nc.scalar.activation(phi_hi[:, k * P:(k + 1) * P], phi_raw[:, k % 2, :], ACT.Identity,
                                         bias=bias[:, 1:2]).then_inc(phi_hi_made, 1)
                    if k == 0:
                        theta_hi(b, 0)
                    if e is not None and k < K - 2:
                        exp_half(e, 1, k + 2)
                if e is not None:
                    exp_hi(e, 0, 0)
                    exp_hi(e, 0, 1)
                    scaled_g_hi(e, 0, 6)
                    scaled_g_hi(e, 0, 7)
                    exp_hi(e, 0, 2)
                    exp_hi(e, 0, 3)

            def main(b=None, v=None):
                for k in range(K):
                    for j in range(J):
                        if v is not None:
                            k2, j2 = (k, j + 2) if j + 2 < J else (k + 1, j + 2 - J)
                            if k2 < K and (k2 > 0 or j2 >= 4):
                                exp_hi(v, k2, j2)
                            if k == HK - 1 and j:
                                scaled_g_hi(v, 1, j - 1)
                            if last_image(v) and k and j == 1:
                                copy_y(v, k - 1)
                        if b is not None:
                            if j == 4 and 1 <= k < K - 1:
                                theta_x_hi(b, k + 1, 1)
                            if v is not None and k >= HK and j in (1, 5):
                                exp_half(b, 0, 2 * (k - HK) + (j == 5))
                    if b is not None and k < K - 1:
                        theta_hi(b, k + 1)
                    if v is not None:
                        if k == HK - 1:
                            scaled_g_hi(v, 1, J - 1)
                        if not last_image(v):
                            copy_y(v, k)
                    if b is not None and k < K - 2:
                        theta_x_hi(b, k + 2, 0)
                    if v is None and k >= HK:
                        exp_half(b, 0, 2 * (k - HK))
                        exp_half(b, 0, 2 * (k - HK) + 1)

            split_weights()
            projections(0)
            main(0)
            projections(1, 0)
            main(1, 0)
            projections(2, 1)
            with act.Fori(2, B - 1) as b:
                main(b, b - 1)
                projections(b + 1, b)
            main(B - 1, B - 2)
            for j in range(4):
                exp_hi(B - 1, 0, j)
            softmax_corrections(B - 1)
            for j in range(J):
                exp_half(B - 1, 1, j)
            for j in range(J):
                scaled_g_hi(B - 1, 0, j)
            main(None, B - 1)
            copy_y(B - 1, K - 1)

            act.wait_ge(bn_img_done, 2 * B + 1)
            nc.scalar.activation(bn_tmp[:, 1, :], bn_tmp[:, 0, :], ACT.Sqrt).then_inc(sqrt_done, 1)

            def y2_hi(t, n):
                act.wait_ge(y2_in[n], t * 16 + 16)
                if not (isinstance(t, int) and t == 0 and n < 2):
                    act.wait_ge(wy2_mm, t * (CH * NBUF) + CH * (n - 1))
                s = 2 * (n % 2)
                nc.scalar.activation(ring_hi[:, s:s + 2, :], y2[n], ACT.Identity).then_inc(y2_hi_made, 1)

            def scale_shift(t, n):
                for c in range(CH):
                    m = CH * n + c
                    act.wait_ge(wy2_mm, t * (CH * NBUF) + (m + 1))
                    nc.scalar.activation(pairs[m % 4], pairs[m % 4], ACT.Identity, bias=bn_shift[:, c:c + 1],
                                         scale=bn_scale[:, c:c + 1]).then_inc(wy2_scaled, 1)

            def store(t, n):
                b = t * IMGS + n // NQ
                q = n % NQ
                act.wait_ge(x_added, t * (CH * NBUF) + (CH * n + CH))
                for c in range(CH):
                    act.dma_start(out_v[b, :, c, q * QT:(q + 1) * QT].rearrange("p (h n) -> p h n", h=2),
                                  x2[n][c]).then_inc(out_done[n], 16)

            def second(t, first=False, last=False):
                for n in range(NBUF):
                    if n < NBUF - 1:
                        y2_hi(t, n + 1)
                    elif not last:
                        y2_hi(t + 1, 0)
                    scale_shift(t, n)
                    if n:
                        store(t, n - 1)
                    elif not first:
                        store(t - 1, NBUF - 1)

            y2_hi(0, 0)
            act.wait_ge(affine_ready, 1)
            second(0, first=True)
            with act.Fori(1, ROUNDS - 1) as t:
                second(t)
            second(ROUNDS - 1, last=True)
            store(ROUNDS - 1, NBUF - 1)

        @block.vector
        def _(dve):
            def low_of_weights():
                dve.wait_ge(w_split_hi, 1)
                nc.vector.tensor_tensor(w_lo[:, :, :, :], w_stage, f32(w_hi[:, :, :, :]),
                                        ALU.subtract).then_inc(w_split_lo, 1)
                dve.wait_ge(w_split_hi, 2)
                nc.vector.tensor_tensor(W_lo[:, :], W_stage, f32(W_hi[:, :]), ALU.subtract).then_inc(w_split_lo, 1)
                nc.vector.memset(tokens[:, :, :], float(N)).then_inc(w_split_lo, 1)
                dve.wait_ge(w_split_lo, 3)

            def proj_x_hi(b, k):
                wait_x_in(dve, b, k)
                wait_proj_x_free(dve, b, k)
                hi, lo = proj_x(k)
                nc.vector.tensor_copy(hi, x_raw[:, BUF[k], :, :]).then_inc(xhi_proj, 1)
                if k in DVE_X:
                    wait(dve, xhi_proj, blk(b, k) + 1)
                    nc.vector.tensor_tensor(lo[:, 1, :], x_raw[:, BUF[k], 1, :], f32(hi[:, 1, :]),
                                            ALU.subtract).then_inc(xlo_proj_dve, 1)

            window = "p (h a w t) -> p h w a t"
            sizes = dict(a=2, w=ROW // 2, t=2)

            def pool_phi(b, k):
                if k >= 2:
                    wait(dve, phi_lo_made, blk(b, k - 1))
                wait(dve, phi_mm, blk(b, k) + 1)
                nc.vector.tensor_reduce(phi_raw[:, k % 2, :].rearrange("p (h w) -> p h w", w=ROW // 2),
                                        f_ps[:, 2 * (k % 2), :].rearrange(window, **sizes), AX.XY,
                                        ALU.max).then_inc(phi_pooled, 1)

            def pool_g(b, k):
                if k >= 2:
                    wait(dve, gT_mm, blk(b, k - 1))
                wait(dve, g_mm, blk(b, k) + 1)
                nc.vector.tensor_reduce(g_raw[:, k % 2, :].rearrange("p (h w) -> p h w", w=ROW // 2),
                                        f_ps[:, 2 * (k % 2) + 1, :].rearrange(window, **sizes), AX.XY,
                                        ALU.max).then_inc(g_pooled, 1)

            def phi_low(b, k):
                wait(dve, phi_hi_made, blk(b, k) + 1)
                wait(dve, phi_pooled, blk(b, k) + 1)
                cols = slice(k * P, (k + 1) * P)
                nc.vector.scalar_tensor_tensor(phi_lo[:, cols], phi_raw[:, k % 2, :], bias[:, 1:2],
                                               f32(phi_hi[:, cols]), ALU.add, ALU.subtract).then_inc(phi_lo_made, 1)

            def copy_gT(b, k):
                wait(dve, gT_mm, blk(b, k) + 1)
                nc.vector.tensor_tensor(gT[:, par(b), k, :], y_ps[:, 0:P], g_bias[:, :],
                                        ALU.add).then_inc(gT_copied, 1)

            def theta_lo(b, k):
                wait(dve, th_hi_made, blk(b, k) + 1)
                hi, lo = theta_tile(b, k)
                nc.vector.scalar_tensor_tensor(lo, t_ps, bias[:, 0:1], f32(hi),
                                               ALU.add, ALU.subtract).then_inc(th_lo_made, 1)

            def store_f(b, k, j, v):
                wait(dve, f_mm, tile(b, k, j) + 1)
                if v is not None:
                    wait_p_lo(dve, v, k, j)
                if j == 0:
                    wait(dve, max_made, 2 * b + k // HK)
                nc.vector.tensor_scalar(exp_tile(k, j), f_ps[:, j % 4, :], 1.0, None, ALU.mult, ALU.max,
                                        accum_out=block_max[:, j, k:k + 1]).then_inc(f_stored, 1)

            def exp_lo(v, k, j):
                if j in POOL_J:
                    return
                wait(dve, p_hi_made, tile(v, k, j) + 1)
                nc.vector.tensor_tensor(ring_lo[:, slot(j), :], exp_tile(k, j), f32(ring_hi[:, slot(j), :]),
                                        ALU.subtract).then_inc(p_lo_dve, 1)

            def half_max(b, h):
                wait(dve, f_stored, tile(b, (h + 1) * HK, 0))
                wait(dve, exp_done, b * (2 * J))
                wait(dve, shift_made, b * 2)
                nc.vector.tensor_reduce(neg_max[:, h, :], block_max[:, :, h * HK:(h + 1) * HK], AX.X, ALU.max,
                                        negate=True).then_inc(max_made, 1)

            def max_shift(b):
                wait(dve, max_made, 2 * b + 2)
                wait(dve, corr_made, b)
                nc.vector.tensor_tensor(neg_all[:, :], neg_max[:, 0, :], neg_max[:, 1, :],
                                        ALU.min).then_inc(shift_made, 1)
                wait(dve, shift_made, 2 * b + 1)
                for h in range(2):
                    last = nc.vector.tensor_tensor(shift_h[:, h, :], neg_all[:, :], neg_max[:, h, :], ALU.subtract)
                last.then_inc(shift_made, 1)

            def softmax_factors(b):
                wait(dve, exp_done, (b + 1) * (2 * J))
                wait(dve, corr_made, b + 1)
                wait(dve, gn_lo_made, b * (2 * J))
                nc.vector.tensor_tensor(part_sum[:, :, :], half_sum[:, :, :], corr[:, :, :],
                                        ALU.mult).then_inc(chain, 1)
                wait(dve, chain, 3 * b + 1)
                nc.vector.tensor_tensor(total[:, :], part_sum[:, 0, :], part_sum[:, 1, :], ALU.add).then_inc(chain, 1)
                wait(dve, chain, 3 * b + 2)
                nc.vector.reciprocal(inv_total[:, :], total[:, :]).then_inc(chain, 1)
                wait(dve, chain, 3 * b + 3)
                for h in range(2):
                    last = nc.vector.tensor_tensor(factor[:, h, :], corr[:, h, :], inv_total[:, :], ALU.mult)
                last.then_inc(factor_made, 1)

            def scaled_g_lo(v, h, j):
                if j == 0:
                    wait(dve, factor_made, v + 1)
                wait(dve, gn_hi_made, v * (2 * J) + (h * J + j + 1))
                nc.vector.scalar_tensor_tensor(gn_lo[:, j, :], gT[:, par(v), j, :], factor[:, h, j:j + 1],
                                               f32(gn_hi[:, j, :]), ALU.mult, ALU.subtract).then_inc(gn_lo_made, 1)

            def y_low(v, k):
                wait(dve, y_hi_made, blk(v, k) + 1)
                nc.vector.tensor_tensor(y_lo[:, :], y32[:, :], f32(y_hi[:, :]),
                                        ALU.subtract).then_inc(y_lo_made, 1)

            def block_stats(v, k):
                wait(dve, wy_mm, blk(v, k) + 1)
                if k == 0:
                    wait(dve, bn_img_done, 2 * v)
                for c in range(CH):
                    last = nc.vector.bn_stats(bn_blk[:, c, k, :], wy_ps[:, c, :])
                last.then_inc(bn_done, 1)

            def image_stats(v):
                wait(dve, bn_done, blk(v, K))
                nc.vector.tensor_scalar(bn_all[:, :, bass.ds(v, 1), 0], tokens[:, :, :], 1.0, None, ALU.mult)
                for c in range(CH):
                    last = nc.vector.bn_aggr(bn_img[:, c, :], bn_blk[:, c, :, :])
                last.then_inc(bn_img_done, 1)
                wait(dve, bn_img_done, 2 * v + 1)
                nc.vector.tensor_copy(bn_all[:, :, bass.ds(v, 1), 1], bn_img[:, :, 0:1])
                nc.vector.tensor_scalar(bn_all[:, :, bass.ds(v, 1), 2], bn_img[:, :, 1:2], float(N), None,
                                        ALU.mult).then_inc(bn_img_done, 1)

            def projections(b, e=None, v=None):
                proj_x_hi(b, 0)
                if e is not None:
                    half_max(e, 1)
                    max_shift(e)
                if v is not None:
                    y_low(v, K - 1)
                    block_stats(v, K - 2)
                proj_x_hi(b, 1)
                for k in range(K):
                    if k < K - 2:
                        proj_x_hi(b, k + 2)
                    if k >= 1:
                        phi_low(b, k - 1)
                    pool_phi(b, k)
                    if e is not None and k == K - 2:
                        softmax_factors(e)
                    if e is not None and k == K - 1:
                        scaled_g_lo(e, 0, 0)
                        scaled_g_lo(e, 0, 1)
                    pool_g(b, k)
                    if k >= 1:
                        copy_gT(b, k - 1)
                    if k == 0:
                        theta_lo(b, 0)
                    if v is not None:
                        if k == 4:
                            block_stats(v, K - 1)
                        if k == 5:
                            image_stats(v)
                phi_low(b, K - 1)
                copy_gT(b, K - 1)
                if e is not None:
                    exp_lo(e, 0, 0)
                    scaled_g_lo(e, 0, 2)
                    scaled_g_lo(e, 0, 3)

            def main(b=None, v=None):
                for k in range(K):
                    for j in range(J):
                        if v is not None:
                            k2, j2 = (k, j + 1) if j + 1 < J else (k + 1, 0)
                            if k2 < K:
                                exp_lo(v, k2, j2)
                        if v is None and j == J - 1 and k < K - 1:
                            theta_lo(b, k + 1)
                        if b is not None:
                            store_f(b, k, j, v)
                        if v is not None:
                            if k == 0 and j < 4:
                                scaled_g_lo(v, 0, j + 4)
                            if j == (3 if last_image(v) else 1) and k >= 1:
                                y_low(v, k - 1)
                            if j == (1 if last_image(v) else 3) and k >= 2:
                                block_stats(v, k - 2)
                            if k == HK - 1 and j >= 2:
                                scaled_g_lo(v, 1, j - 2)
                    if b is not None and v is not None and k < K - 1:
                        theta_lo(b, k + 1)
                    if v is not None and k == HK - 1:
                        scaled_g_lo(v, 1, J - 2)
                        scaled_g_lo(v, 1, J - 1)
                    if b is not None and k == HK - 1:
                        half_max(b, 0)

            low_of_weights()
            projections(0)
            main(0)
            projections(1, 0)
            main(1, 0)
            projections(2, 1, 0)
            with dve.Fori(2, B - 1) as b:
                main(b, b - 1)
                projections(b + 1, b, b - 1)
            main(B - 1, B - 2)
            half_max(B - 1, 1)
            max_shift(B - 1)
            y_low(B - 2, K - 1)
            block_stats(B - 2, K - 2)
            block_stats(B - 2, K - 1)
            image_stats(B - 2)
            exp_lo(B - 1, 0, 0)
            softmax_factors(B - 1)
            for j in range(4):
                scaled_g_lo(B - 1, 0, j)
            main(None, B - 1)
            y_low(B - 1, K - 1)
            block_stats(B - 1, K - 2)
            block_stats(B - 1, K - 1)
            image_stats(B - 1)

            count = [0]

            def link(instruction):
                count[0] += 1
                instruction.then_inc(chain, 1)
                dve.wait_ge(chain, 3 * B + count[0])

            dve.wait_ge(bn_img_done, 2 * B)
            for c in range(CH):
                link(nc.vector.bn_aggr(bn_tot[:, c, :], bn_all[:, c, :, :]))
            var_eps, root, guess, mean_all, tmp, tmp2 = (bn_tmp[:, i, :] for i in range(6))
            nc.vector.tensor_scalar(var_eps, bn_tot[:, :, 1], BN_EPS, None, ALU.add).then_inc(bn_img_done, 1)
            dve.wait_ge(sqrt_done, 1)
            link(nc.vector.reciprocal(guess, root))
            link(nc.vector.tensor_tensor(tmp, guess, guess, ALU.mult))
            link(nc.vector.tensor_tensor(tmp2, tmp, var_eps, ALU.mult))
            link(nc.vector.tensor_scalar(tmp, tmp2, -0.5, 1.5, ALU.mult, ALU.add))
            link(nc.vector.tensor_tensor(tmp2, guess, tmp, ALU.mult))
            link(nc.vector.tensor_tensor(bn_scale[:, :], tmp2, chans[:, :, 1], ALU.mult))
            link(nc.vector.tensor_tensor(mean_all, bn_tot[:, :, 0], chans[:, :, 0], ALU.add))
            link(nc.vector.tensor_tensor(tmp, chans[:, :, 0], mean_all, ALU.subtract))
            link(nc.vector.tensor_tensor(tmp2, tmp, bn_scale[:, :], ALU.mult))
            nc.vector.tensor_tensor(bn_shift[:, :], tmp2, chans[:, :, 2], ALU.add).then_inc(affine_ready, 1)

            def y2_lo(t, n):
                dve.wait_ge(y2_hi_made, t * NBUF + (n + 1))
                s = 2 * (n % 2)
                nc.vector.tensor_tensor(ring_lo[:, s:s + 2, :], y2[n], f32(ring_hi[:, s:s + 2, :]),
                                        ALU.subtract).then_inc(y2_lo_made, 1)

            def add_x(t, n):
                dve.wait_ge(x2_in[n], t * (16 * CH) + 16 * CH)
                for c in range(CH):
                    m = CH * n + c
                    dve.wait_ge(wy2_scaled, t * (CH * NBUF) + (m + 1))
                    nc.vector.tensor_tensor(x2[n][c], pairs[m % 4], x2[n][c], ALU.add).then_inc(x_added, 1)

            def second(t, last=False):
                for n in range(NBUF):
                    if n < NBUF - 1:
                        y2_lo(t, n + 1)
                    elif not last:
                        y2_lo(t + 1, 0)
                    add_x(t, n)

            y2_lo(0, 0)
            second(0)
            with dve.Fori(1, ROUNDS - 1) as t:
                second(t)
            second(ROUNDS - 1, last=True)

        @block.gpsimd
        def _(pool):
            def proj_x_lo(b, k):
                hi, lo = proj_x(k)
                wait(pool, xhi_proj, blk(b, k) + 1)
                for c in range(1 if k in DVE_X else CH):
                    last = nc.gpsimd.tensor_tensor(lo[:, c, :], x_raw[:, BUF[k], c, :], f32(hi[:, c, :]), ALU.subtract)
                last.then_inc(xlo_proj, 1)

            def theta_x_lo(b, k, c):
                wait(pool, xhi_theta, b * (2 * (K - 2)) + (2 * (k - 2) + c + 1))
                nc.gpsimd.tensor_tensor(xm_lo[:, :], x_raw[:, BUF[K + k - 2], c, :], f32(xm_hi[:, :]),
                                        ALU.subtract).then_inc(xlo_theta, 1)

            def projections(b):
                for k in range(K):
                    proj_x_lo(b, k)

            def main(b=None, v=None):
                for k in range(K):
                    for n, j in enumerate(POOL_J):
                        if v is not None:
                            wait(pool, p_hi_made, tile(v, k, j) + 1)
                            nc.gpsimd.tensor_tensor(ring_lo[:, slot(j), :], exp_tile(k, j),
                                                    f32(ring_hi[:, slot(j), :]),
                                                    ALU.subtract).then_inc(p_lo_pool, 1)
                        if b is not None and 1 <= k < K - 1:
                            if n == 0:
                                theta_x_lo(b, k + 1, 0)
                            if n == 2:
                                theta_x_lo(b, k + 1, 1)

            projections(0)
            main(0)
            projections(1)
            main(1, 0)
            projections(2)
            with pool.Fori(2, B - 1) as b:
                main(b, b - 1)
                projections(b + 1)
            main(B - 1, B - 2)
            main(None, B - 1)


def kernel(**inputs):
    import numpy as np
    import concourse.bacc as bacc
    from concourse import mybir as mb
    from concourse.bass_utils import run_bass_kernel_spmd as run

    def arr(name):
        return np.asarray(inputs[name])

    x = np.ascontiguousarray(arr("x"))
    B, C, H, W = x.shape
    arrays = {
        "x_dram": x.reshape(B, C, H * W),
        "wT_dram": np.ascontiguousarray(np.stack([arr(f"L0_conv_{n}_w").T for n in ("theta", "phi", "g")], axis=1)),
        "bias_dram": np.ascontiguousarray(np.stack([arr(f"L0_conv_{n}_b") for n in ("theta", "phi")], axis=1)),
        "g_bias_dram": np.ascontiguousarray(np.broadcast_to(arr("L0_conv_g_b"), (128, arr("L0_conv_g_b").size))),
        "WT_dram": np.ascontiguousarray(arr("L0_conv_W_w").T),
        "chan_dram": np.ascontiguousarray(
            np.stack([arr(f"L0_conv_{n}") for n in ("W_b", "bn_gamma", "bn_beta")], axis=1)),
        "ident_dram": np.eye(128, dtype=np.float32),
    }
    IC = arrays["WT_dram"].shape[0]
    nc = bacc.Bacc("TRN2", target_bir_lowering=False, num_devices=1)
    args = [nc.dram_tensor(n, a.shape, mb.dt.from_np(a.dtype), kind="ExternalInput").ap() for n, a in arrays.items()]
    out = nc.dram_tensor("out_dram", (B, C, H * W), mb.dt.float32, kind="ExternalOutput").ap()
    y = nc.dram_tensor("y_dram", (B, IC, H * W), mb.dt.float32).ap()
    nonlocal_block_kernel(nc, *args, out, y)
    r = run(nc, [arrays], core_ids=[0])
    return r.results[0]["out_dram"].reshape(B, C, H, W)
```

```python
from contextlib import ExitStack

import concourse.bass as bass
from concourse import mybir

F32 = mybir.dt.float32
F32R = mybir.dt.float32r
ALU = mybir.AluOpType
ACT = mybir.ActivationFunctionType
AX = mybir.AxisListType

P = 128
NB = 512
BN_EPS = 1e-05

POOL_J = (1, 3, 5, 7)
DVE_X = (0, 1)


def nonlocal_block_kernel(nc, x, wT, biases, g_bias_rows, WT, chan, ident_in, out, y_dram):
    B, C, N = x.shape[0], x.shape[1], x.shape[2]
    CH = C // P
    IC = WT.shape[0]
    K = N // NB
    S = N // 4
    J = S // P
    ROW = 64
    HK = K // 2
    HN = HK * NB
    assert IC == P and C == 2 * P and J == K == 8 and N == K * NB
    NPOOL = len(POOL_J)
    NDVE = J - NPOOL

    x_v = x.rearrange("b (c p) n -> b p c n", p=P)
    out_v = out.rearrange("b (c p) n -> b p c n", p=P)

    ctx = ExitStack()
    with ctx:
        def sb(name, shape, dt=F32):
            return ctx.enter_context(nc.sbuf_tensor(name, shape, dt))

        def ps(name, shape):
            return ctx.enter_context(nc.psum_tensor(name, shape, F32))

        def sem(name):
            return ctx.enter_context(nc.semaphore(name))

        scores = sb("scores", [P, J, N])
        ring_hi = sb("ring_hi", [P, 4, NB], F32R)
        ring_lo = sb("ring_lo", [P, 4, NB], F32R)
        x_raw = sb("x_raw", [P, 3, CH, NB])
        xm_hi = sb("xm_hi", [P, NB], F32R)
        xm_lo = sb("xm_lo", [P, NB], F32R)
        th_hi = sb("th_hi", [P, NB], F32R)
        th_lo = sb("th_lo", [P, NB], F32R)
        phi_hi = sb("phi_hi", [P, S], F32R)
        phi_lo = sb("phi_lo", [P, S], F32R)
        phi_raw = sb("phi_raw", [P, 2, P])
        g_raw = sb("g_raw", [P, 2, P])
        g_bias = sb("g_bias", [P, P])
        gT = sb("gT", [P, 2, J, P])
        gn_hi = sb("gn_hi", [P, J, P], F32R)
        gn_lo = sb("gn_lo", [P, J, P], F32R)
        w_hi = sb("w_hi", [P, CH, 3, P], F32R)
        w_lo = sb("w_lo", [P, CH, 3, P], F32R)
        W_hi = sb("W_hi", [P, C], F32R)
        W_lo = sb("W_lo", [P, C], F32R)
        y32 = sb("y32", [P, NB])
        y_hi = sb("y_hi", [P, NB], F32R)
        y_lo = sb("y_lo", [P, NB], F32R)
        ident = sb("ident", [P, P])
        bias = sb("bias", [P, 2])
        chans = sb("chans", [P, CH, 3])
        block_max = sb("block_max", [P, J, K])
        neg_max = sb("neg_max", [P, 2, J])
        half_sum = sb("half_sum", [P, 2, J])
        neg_all = sb("neg_all", [P, J])
        shift_h = sb("shift_h", [P, 2, J])
        corr = sb("corr", [P, 2, J])
        part_sum = sb("part_sum", [P, 2, J])
        total = sb("total", [P, J])
        inv_total = sb("inv_total", [P, J])
        factor = sb("factor", [P, 2, J])
        bn_blk = sb("bn_blk", [P, CH, K, 6])
        bn_img = sb("bn_img", [P, CH, 2])
        bn_all = sb("bn_all", [P, CH, B, 3])
        tokens = sb("tokens", [P, CH, 1])
        bn_tot = sb("bn_tot", [P, CH, 2])
        bn_tmp = sb("bn_tmp", [P, 8, CH])
        bn_scale = sb("bn_scale", [P, CH])
        bn_shift = sb("bn_shift", [P, CH])

        w_stage = scores[:, 0, 0:CH * 3 * P].rearrange("p (c t i) -> p c t i", c=CH, t=3)
        W_stage = scores[:, 0, 1024:1024 + C]
        QT = 2 * NB
        NQ = N // QT
        NBUF = K
        IMGS = NBUF // NQ
        NEXTRA = NQ
        ROUNDS, REST = divmod((B - 1) * NQ, NBUF)
        assert ROUNDS >= 2 and 0 < REST and CH * 2 + 2 <= J - 2
        x2 = [[scores[:, 2 * c:2 * c + 2, n * NB:(n + 1) * NB] for c in range(CH)] for n in range(NBUF)]
        y2 = [scores[:, 2 * CH:2 * CH + 2, n * NB:(n + 1) * NB] for n in range(NBUF)]
        spare = [x_raw[:, u, :, :] for u in range(3)]
        spare += [gT[:, B % 2, :, :].rearrange("p (h a) i -> p h (a i)", h=2)]
        spare += [scores[:, J - 2:J, n * NB:(n + 1) * NB] for n in range(K)]
        y2 += [spare[3 * e] for e in range(NEXTRA)]
        x2 += [spare[3 * e + 1:3 * e + 3] for e in range(NEXTRA)]
        assert len(spare) == (CH + 1) * NEXTRA

        f_ps = ps("f_ps", [P, 4, NB])
        ty_ps = ps("ty_ps", [P, 2, NB])
        t_ps = ty_ps[:, 0, :]
        y_ps = ty_ps[:, 1, :]
        wy_ps = ps("wy_ps", [P, CH, NB])
        pairs = [f_ps[:, 0:2, :], f_ps[:, 2:4, :], ty_ps[:, :, :], wy_ps[:, :, :]]

        w_in = sem("w_in")
        ident_arrived = sem("ident_arrived")
        W_arrived = sem("W_arrived")
        w_split_hi = sem("w_split_hi")
        w_split_lo = sem("w_split_lo")
        x_in = [sem(f"x_in{i}") for i in range(3)]
        y_out = sem("y_out")
        xhi_proj = sem("xhi_proj")
        xhi_theta = sem("xhi_theta")
        xlo_proj = sem("xlo_proj")
        xlo_proj_dve = sem("xlo_proj_dve")
        xlo_theta = sem("xlo_theta")
        theta_half_mm = sem("theta_half_mm")
        phi_mm = sem("phi_mm")
        g_mm = sem("g_mm")
        gT_mm = sem("gT_mm")
        theta_mm = sem("theta_mm")
        f_mm = sem("f_mm")
        y_mm = sem("y_mm")
        wy_mm = sem("wy_mm")
        phi_pooled = sem("phi_pooled")
        g_pooled = sem("g_pooled")
        phi_hi_made = sem("phi_hi_made")
        phi_lo_made = sem("phi_lo_made")
        gT_copied = sem("gT_copied")
        th_hi_made = sem("th_hi_made")
        th_lo_made = sem("th_lo_made")
        f_stored = sem("f_stored")
        max_made = sem("max_made")
        exp_done = sem("exp_done")
        shift_made = sem("shift_made")
        corr_made = sem("corr_made")
        factor_made = sem("factor_made")
        chain = sem("chain")
        gn_hi_made = sem("gn_hi_made")
        gn_lo_made = sem("gn_lo_made")
        p_hi_made = sem("p_hi_made")
        p_lo_dve = sem("p_lo_dve")
        p_lo_pool = sem("p_lo_pool")
        y_copied = sem("y_copied")
        y_hi_made = sem("y_hi_made")
        y_lo_made = sem("y_lo_made")
        bn_done = sem("bn_done")
        bn_img_done = sem("bn_img_done")
        sqrt_done = sem("sqrt_done")
        affine_ready = sem("affine_ready")
        x2_in = [sem(f"x2_in{n}") for n in range(NBUF + NEXTRA)]
        y2_in = [sem(f"y2_in{n}") for n in range(NBUF + NEXTRA)]
        out_done = [sem(f"out_done{n}") for n in range(NBUF + NEXTRA)]
        y2_hi_made = sem("y2_hi_made")
        y2_lo_made = sem("y2_lo_made")
        wy2_mm = sem("wy2_mm")
        wy2_scaled = sem("wy2_scaled")
        x_added = sem("x_added")

        def blk(b, k):
            return b * K + k

        def tile(b, k, j):
            return b * (K * J) + (k * J + j)

        def par(b):
            return b % 2

        def wait(eng, s, value):
            if not isinstance(value, int) or value > 0:
                eng.wait_ge(s, value)

        def wait_p_lo(eng, v, k, j):
            if j in POOL_J:
                wait(eng, p_lo_pool, blk(v, k) * NPOOL + (POOL_J.index(j) + 1))
            else:
                wait(eng, p_lo_dve, blk(v, k) * NDVE + (j - sum(q < j for q in POOL_J) + 1))

        def slot(j):
            return j % 4

        ORDER = (0, K - 1) + tuple(range(1, K - 1))

        LOADS = K + K - 2
        BUF = [(i + 1) % 3 if i < K else (i - K) % 3 for i in range(LOADS)]

        def former_load(i):
            former = [q for q in range(i) if BUF[q] == BUF[i]]
            return former[-1] if former else None

        HALVED = [former_load(i) in DVE_X for i in range(LOADS)]

        def arrivals(u, n):
            return sum(32 if HALVED[q] else 16 for q in range(n) if BUF[q] == u)

        def wait_x_in(eng, b, i):
            u = BUF[i]
            eng.wait_ge(x_in[u], b * arrivals(u, LOADS) + arrivals(u, i + 1))

        def wait_x_lo(eng, b, i):
            if i < K:
                eng.wait_ge(xlo_proj, blk(b, i) + 1)
                if i in DVE_X:
                    eng.wait_ge(xlo_proj_dve, b * len(DVE_X) + (DVE_X.index(i) + 1))
            else:
                eng.wait_ge(xlo_theta, b * (2 * (K - 2)) + 2 * (i - K + 1))

        PLACE = (0, 1, "G", 0, 1, "G", 0, 1)

        def proj_x(k):
            if PLACE[k] == "G":
                return tuple(t[:, :, :].rearrange("p (c a) i -> p c (a i)", c=CH) for t in (gn_hi, gn_lo))
            s = 2 * PLACE[k]
            return ring_hi[:, s:s + 2, :], ring_lo[:, s:s + 2, :]

        def wait_proj_x_free(eng, b, k):
            former = [q for q in range(k) if PLACE[q] == PLACE[k]]
            if former:
                wait(eng, g_mm, blk(b, former[-1] + 1))
                if former[-1] == 0:
                    wait(eng, theta_mm, blk(b, 0) + 1)
            elif not (isinstance(b, int) and b < 2):
                wait(eng, y_mm, tile(b - 1, 0, 0) - (2 if PLACE[k] == 0 else 0))
            elif isinstance(b, int) and b == 1 and PLACE[k] == 1:
                wait(eng, f_mm, tile(1, 0, 0))

        def exp_tile(k, j):
            return scores[:, j, k * NB:(k + 1) * NB]

        def first_image(b):
            return isinstance(b, int) and b == 0

        def last_image(v):
            return isinstance(v, int) and v == B - 1

        def theta_tile(b, k):
            if first_image(b) and k % 2:
                return ring_hi[:, 3, :], ring_lo[:, 3, :]
            return th_hi[:, :], th_lo[:, :]

        def y_bank(v, k):
            return t_ps if last_image(v) and k % 2 else y_ps

        FIRST = [(0, n) for e in range(NEXTRA) for n in (e, NBUF + e)] + [(0, n) for n in range(NEXTRA, NBUF)]

        def round_of(t):
            return [(t, n) for n in range(NBUF)]

        LAST = [(ROUNDS, n) for n in range(REST)]

        def before(t, n):
            return FIRST.index((t, n)) if isinstance(t, int) and t == 0 else t * NBUF + (NEXTRA + n)

        def turn(t, n):
            assert NBUF % 2 == 0 and NEXTRA % 2 == 0
            return (before(t, n) if isinstance(t, int) else n) % 2

        def in_dram(t, n):
            b = 0 if n >= NBUF else t * IMGS + (1 + n // NQ)
            q = n % NQ
            return b, slice(q * QT, (q + 1) * QT)

        def f32(ap):
            return ap.bitcast(F32)

        block = ctx.enter_context(nc.Block())

        @block.sync
        def _(sp):
            sp.dma_start(w_stage, wT.rearrange("(c p) t i -> p c t i", p=P)).then_inc(w_in, 16)
            sp.dma_start(bias[:, :], biases).then_inc(w_in, 16)
            sp.dma_start(g_bias[:, :], g_bias_rows).then_inc(w_in, 16)

            def load(b, i):
                k = i if i < K else ORDER[i - K + 2]
                cols = slice(k * NB, (k + 1) * NB)
                former = former_load(i)
                if HALVED[i]:
                    sp.wait_ge(xlo_proj, blk(b, former) + 1)
                    sp.dma_start(x_raw[:, BUF[i], 0, :], x_v[b, :, 0, cols]).then_inc(x_in[BUF[i]], 16)
                    sp.wait_ge(xlo_proj_dve, b * len(DVE_X) + (DVE_X.index(former) + 1))
                    sp.dma_start(x_raw[:, BUF[i], 1, :], x_v[b, :, 1, cols]).then_inc(x_in[BUF[i]], 16)
                    return
                if former is not None:
                    wait_x_lo(sp, b, former)
                elif not (isinstance(b, int) and b == 0):
                    wait_x_lo(sp, b - 1, max(q for q in range(LOADS) if BUF[q] == BUF[i]))
                sp.dma_start(x_raw[:, BUF[i], :, :], x_v[b, :, :, cols]).then_inc(x_in[BUF[i]], 16)

            load(0, 0)
            sp.dma_start(ident[:, :], ident_in).then_inc(ident_arrived, 16)
            load(0, 1)
            sp.dma_start(W_stage, WT).then_inc(W_arrived, 16)
            sp.dma_start(chans[:, :, :], chan.rearrange("(c p) t -> p c t", p=P)).then_inc(W_arrived, 16)
            for i in range(2, LOADS):
                load(0, i)
            with sp.Fori(1, B) as b:
                for i in range(LOADS):
                    load(b, i)

            def load2(t, n, part):
                b, cols = in_dram(t, n)
                if part == 0:
                    sp.dma_start(y2[n], y_dram[b, :, cols].rearrange("p (h n) -> p h n", h=2)).then_inc(y2_in[n], 16)
                else:
                    sp.dma_start(x2[n][part - 1],
                                 x_v[b, :, part - 1, cols].rearrange("p (h n) -> p h n", h=2)).then_inc(x2_in[n], 16)

            def load_spare(i):
                e, part = divmod(i, CH + 1)
                load2(0, NBUF + e, part)

            sp.wait_ge(y_out, 16 * ((1 + IMGS) * K))
            sp.wait_ge(xlo_theta, B * (2 * (K - 2)))
            sp.wait_ge(gn_lo_made, (B - 1) * (2 * J))
            for i in range(len(spare) - K):
                load_spare(i)
            for n in range(NBUF):
                sp.wait_ge(p_lo_pool, (blk(B - 1, n) + 1) * NPOOL)
                sp.wait_ge(p_lo_dve, (blk(B - 1, n) + 1) * NDVE)
                for part in range(CH + 1):
                    load2(0, n, part)
                load_spare(len(spare) - K + n)
            sp.wait_ge(y_out, 16 * (B * K))
            with sp.Fori(1, ROUNDS) as t:
                for _, n in round_of(t):
                    sp.wait_ge(out_done[n], t * (16 * CH))
                    for part in range(CH + 1):
                        load2(t, n, part)
            for t, n in LAST:
                sp.wait_ge(out_done[n], t * (16 * CH))
                for part in range(CH + 1):
                    load2(t, n, part)
            for n in range(NBUF + NEXTRA):
                stores = 1 if n >= NBUF else ROUNDS + (n < REST)
                sp.wait_ge(out_done[n], stores * (16 * CH))

        @block.tensor
        def _(pe):
            def split_product(acc, parts, start, stop):
                last = None
                n = len(parts)
                for i, (a_hi, a_lo, m_hi, m_lo) in enumerate(parts):
                    nc.tensor.matmul(acc, a_lo, m_hi, start=start and i == 0, stop=False)
                    nc.tensor.matmul(acc, a_hi, m_lo, start=False, stop=False)
                    last = nc.tensor.matmul(acc, a_hi, m_hi, start=False, stop=stop and i == n - 1)
                return last

            def weights(t, x_hi, x_lo):
                return [(w_hi[:, c, t, :], w_lo[:, c, t, :], x_hi[:, c, :], x_lo[:, c, :]) for c in range(CH)]

            def project(b, k):
                wait_x_lo(pe, b, k)
                bank = 2 * (k % 2)
                if k < 2:
                    wait(pe, f_stored, tile(b, 0, 0) - (2 - 2 * k) if not isinstance(b, int) or b else 0)
                else:
                    wait(pe, phi_pooled, blk(b, k - 1))
                    wait(pe, g_pooled, blk(b, k - 1))
                x_hi, x_lo = proj_x(k)
                split_product(f_ps[:, bank, :], weights(1, x_hi, x_lo), True, True).then_inc(phi_mm, 1)
                split_product(f_ps[:, bank + 1, :], weights(2, x_hi, x_lo), True, True).then_inc(g_mm, 1)

            def transpose_g(b, k):
                wait(pe, g_pooled, blk(b, k) + 1)
                if k:
                    wait(pe, gT_copied, blk(b, k))
                elif not (isinstance(b, int) and b < 2):
                    wait(pe, y_copied, blk(b - 1, 0))
                nc.tensor.matmul(y_ps[:, 0:P], g_raw[:, k % 2, :], ident[:, :], start=True, stop=True,
                                 is_transpose=True).then_inc(gT_mm, 1)

            def theta_early(b, k):
                wait(pe, th_lo_made, blk(b, k))
                x_hi, x_lo = proj_x(ORDER[k])
                split_product(t_ps, weights(0, x_hi, x_lo), True, True).then_inc(theta_mm, 1)

            def theta_half(b, k, c):
                wait(pe, xlo_theta, b * (2 * (K - 2)) + (2 * (k - 2) + c + 1))
                if c == 0:
                    wait(pe, th_lo_made, blk(b, k))
                split_product(t_ps, [(w_hi[:, c, 0, :], w_lo[:, c, 0, :], xm_hi[:, :], xm_lo[:, :])],
                              c == 0, c == CH - 1).then_inc(theta_mm if c == CH - 1 else theta_half_mm, 1)

            def score(b, k, j):
                if j == 0:
                    wait(pe, th_lo_made, blk(b, k) + 1)
                if k == 0:
                    wait(pe, phi_lo_made, blk(b, j) + 1)
                    if j in (0, 2):
                        wait(pe, g_pooled, blk(b, K - 1 + j // 2))
                if k or j >= 4:
                    wait(pe, f_stored, tile(b, k, j) - 3)
                cols = slice(j * P, (j + 1) * P)
                split_product(f_ps[:, j % 4, :], [(phi_hi[:, cols], phi_lo[:, cols], *theta_tile(b, k))],
                              True, True).then_inc(f_mm, 1)

            def attend(v, k, j):
                if k % HK == 0:
                    wait(pe, gn_lo_made, v * (2 * J) + (k // HK * J + j + 1))
                if j == 0:
                    wait(pe, y_copied, blk(v, max(k - 1, 0)) if last_image(v) else blk(v, k))
                    if last_image(v) and k == 1:
                        wait(pe, th_lo_made, B * K)
                    if k == 0 and not (isinstance(v, int) and v == B - 1):
                        wait(pe, gT_copied, blk(v + 2, 0))
                wait_p_lo(pe, v, k, j)
                s = slot(j)
                split_product(y_bank(v, k), [(gn_hi[:, j, :], gn_lo[:, j, :], ring_hi[:, s, :], ring_lo[:, s, :])],
                              j == 0, j == J - 1).then_inc(y_mm, 1)

            def output_conv(v, k):
                wait(pe, y_lo_made, blk(v, k) + 1)
                wait(pe, bn_done, blk(v, k))
                for c in range(CH):
                    cols = slice(c * P, (c + 1) * P)
                    last = split_product(wy_ps[:, c, :], [(W_hi[:, cols], W_lo[:, cols], y_hi[:, :], y_lo[:, :])],
                                         True, True)
                last.then_inc(wy_mm, 1)

            def projections(b, v=None):
                for k in range(K):
                    project(b, k)
                    if k == 0 and v is not None:
                        output_conv(v, K - 1)
                    if k in ORDER[:2]:
                        theta_early(b, ORDER.index(k))
                    if k:
                        transpose_g(b, k - 1)
                score(b, 0, 0)
                score(b, 0, 1)
                transpose_g(b, K - 1)

            def main(b=None, v=None):
                for k in range(K):
                    for s in range(J + 2):
                        if b is not None and s < J:
                            if k or s >= 2:
                                score(b, k, s)
                            if s == (1 if v is None else 4) and 1 <= k < K - 1:
                                theta_half(b, k + 1, 0)
                        if v is not None:
                            if k == 0 and s == 3:
                                attend(v, k, 0)
                                attend(v, k, 1)
                            elif s >= (4 if k == 0 else 2):
                                attend(v, k, s - 2)
                            if last_image(v) and k and s == J - 2:
                                output_conv(v, k - 1)
                        if b is not None and s == (4 if v is None else J) and 1 <= k < K - 1:
                            theta_half(b, k + 1, 1)
                    if v is not None and k and not last_image(v):
                        output_conv(v, k - 1)

            pe.wait_ge(w_split_lo, 1)
            pe.wait_ge(ident_arrived, 16)
            projections(0)
            main(0)
            projections(1)
            main(1, 0)
            projections(2, 0)
            with pe.Fori(2, B - 1) as b:
                main(b, b - 1)
                projections(b + 1, b - 1)
            main(B - 1, B - 2)
            output_conv(B - 2, K - 1)
            main(None, B - 1)
            output_conv(B - 1, K - 1)


            def output_conv2(t, n):
                pe.wait_ge(y2_lo_made, before(t, n) + 1)
                for c in range(CH):
                    wait(pe, x_added, before(t, n) * CH + (c - 3))
                    for h in range(2):
                        cols = slice(c * P, (c + 1) * P)
                        s = 2 * turn(t, n) + h
                        last = split_product(pairs[CH * turn(t, n) + c][:, h, :],
                                             [(W_hi[:, cols], W_lo[:, cols], ring_hi[:, s, :], ring_lo[:, s, :])],
                                             True, True)
                    last.then_inc(wy2_mm, 1)

            pe.wait_ge(f_stored, tile(B, 0, 0))
            output_conv2(*FIRST[0])
            pe.wait_ge(bn_done, B * K)
            pe.wait_ge(y_copied, B * K)
            pe.wait_ge(th_lo_made, B * K)
            for piece in FIRST[1:]:
                output_conv2(*piece)
            with pe.Fori(1, ROUNDS) as t:
                for piece in round_of(t):
                    output_conv2(*piece)
            for piece in LAST:
                output_conv2(*piece)

        @block.scalar
        def _(act):
            def exp_half(b, h, j):
                if j == 0:
                    wait(act, max_made, 2 * b + (h + 1))
                    wait(act, factor_made, b)
                cols = scores[:, j, h * HN:(h + 1) * HN]
                nc.scalar.activation(cols, cols, ACT.Exp, bias=neg_max[:, h, j:j + 1],
                                     accum_out=half_sum[:, h, j:j + 1]).then_inc(exp_done, 1)

            def exp_hi(v, k, j):
                if k % HK == 0 and j == 0:
                    wait(act, exp_done, v * (2 * J) + (J if k == 0 else 2 * J))
                if k == 0 and j < 4:
                    if not (isinstance(v, int) and v == B - 1):
                        if slot(j) < 2:
                            wait(act, g_mm, blk(v + 1, K - 1))
                        else:
                            wait(act, theta_mm, blk(v + 1, 2))
                    else:
                        wait(act, y_mm, tile(v, 0, j) - 3)
                else:
                    wait(act, y_mm, tile(v, k, j) - 3)
                nc.scalar.activation(ring_hi[:, slot(j), :], exp_tile(k, j), ACT.Identity).then_inc(p_hi_made, 1)

            def theta_x_hi(b, k, c):
                i = K + k - 2
                if c == 0:
                    wait_x_in(act, b, i)
                    wait(act, theta_mm, blk(b, k))
                else:
                    wait(act, theta_half_mm, b * (K - 2) + (k - 1))
                nc.scalar.activation(xm_hi[:, :], x_raw[:, BUF[i], c, :], ACT.Identity).then_inc(xhi_theta, 1)

            def theta_hi(b, k):
                wait(act, theta_mm, blk(b, k) + 1)
                wait(act, f_mm, tile(b, max(k - 1, 0) if first_image(b) else k, 0))
                nc.scalar.activation(theta_tile(b, k)[0], t_ps, ACT.Identity, bias=bias[:, 0:1]).then_inc(th_hi_made, 1)

            def copy_y(v, k):
                wait(act, y_mm, tile(v, k, J))
                wait(act, y_out, v * (16 * K) + 16 * k)
                wait(act, y_lo_made, blk(v, k))
                nc.scalar.copy(y32[:, :], y_bank(v, k)).then_inc(y_copied, 1)
                act.wait_ge(y_copied, blk(v, k) + 1)
                wait(act, wy_mm, blk(v, k))
                nc.scalar.activation(y_hi[:, :], y32[:, :], ACT.Identity).then_inc(y_hi_made, 1)
                act.dma_start(y_dram[v, :, ORDER[k] * NB:(ORDER[k] + 1) * NB], y32[:, :]).then_inc(y_out, 16)

            def scaled_g_hi(v, h, j):
                if j == 0 or (last_image(v) and j == J // 2):
                    wait(act, factor_made, v + (1 if j == 0 else 2))
                    if h == 0 and not (isinstance(v, int) and v == B - 1):
                        wait(act, g_mm, blk(v + 1, 2 + max(q for q in range(K) if PLACE[q] == "G")) - 1)
                wait(act, y_mm, tile(v, HK - 1, j) + 1 if h else tile(v - 1, K - 1, j) + 1
                     if not (isinstance(v, int) and v == 0) else 0)
                nc.scalar.activation(gn_hi[:, j, :], gT[:, par(v), j, :], ACT.Identity,
                                     scale=factor[:, h, j:j + 1]).then_inc(gn_hi_made, 1)

            def split_weights():
                act.wait_ge(w_in, 16 * 3)
                nc.scalar.activation(w_hi[:, :, :, :], w_stage, ACT.Identity).then_inc(w_split_hi, 1)
                act.wait_ge(W_arrived, 16 * 2)
                nc.scalar.activation(W_hi[:, :], W_stage, ACT.Identity).then_inc(w_split_hi, 1)

            def softmax_corrections(e):
                wait(act, shift_made, 2 * e + 2)
                nc.scalar.activation(corr[:, :, :], shift_h[:, :, :], ACT.Exp).then_inc(corr_made, 1)

            def projections(b, e=None):
                if e is not None:
                    exp_half(e, 1, 0)
                    exp_half(e, 1, 1)
                    softmax_corrections(e)
                for k in range(K):
                    if e is not None and k == K - 1:
                        for j in range(6):
                            scaled_g_hi(e, 0, j)
                    wait(act, phi_pooled, blk(b, k) + 1)
                    nc.scalar.activation(phi_hi[:, k * P:(k + 1) * P], phi_raw[:, k % 2, :], ACT.Identity,
                                         bias=bias[:, 1:2]).then_inc(phi_hi_made, 1)
                    if k == 0:
                        theta_hi(b, 0)
                    if e is not None and k < K - 2:
                        exp_half(e, 1, k + 2)
                if e is not None:
                    exp_hi(e, 0, 0)
                    exp_hi(e, 0, 1)
                    scaled_g_hi(e, 0, 6)
                    scaled_g_hi(e, 0, 7)
                    exp_hi(e, 0, 2)
                    exp_hi(e, 0, 3)

            def main(b=None, v=None):
                for k in range(K):
                    for j in range(J):
                        if v is not None:
                            k2, j2 = (k, j + 2) if j + 2 < J else (k + 1, j + 2 - J)
                            if b is not None and j == J - 1 and k < K - 1:
                                theta_hi(b, k + 1)
                            if k2 < K and (k2 > 0 or (j2 >= 4 and not last_image(v))):
                                exp_hi(v, k2, j2)
                            if k == HK - 1 and j:
                                scaled_g_hi(v, 1, j - 1)
                            if last_image(v) and k and j == 1:
                                copy_y(v, k - 1)
                            if last_image(v) and k == 1 and j == 4:
                                act.wait_ge(exp_done, B * (2 * J))
                                nc.scalar.activation(bn_tmp[:, 7, 0:1], half_sum[:, 0, 0:1], ACT.Sqrt)
                        if b is not None:
                            if j == 4 and 1 <= k < K - 1:
                                theta_x_hi(b, k + 1, 1)
                            if k >= HK and j in ((4,) if v is None else (1, 5)):
                                exp_half(b, 0, 2 * (k - HK) + (j == 5))
                    if v is None and k < K - 1:
                        theta_hi(b, k + 1)
                    if v is not None:
                        if k == HK - 1:
                            scaled_g_hi(v, 1, J - 1)
                        if not last_image(v):
                            copy_y(v, k)
                    if b is not None and k < K - 2:
                        theta_x_hi(b, k + 2, 0)
                    if v is None and k >= HK:
                        exp_half(b, 0, 2 * (k - HK) + 1)

            split_weights()
            projections(0)
            main(0)
            projections(1, 0)
            main(1, 0)
            projections(2, 1)
            with act.Fori(2, B - 1) as b:
                main(b, b - 1)
                projections(b + 1, b)
            main(B - 1, B - 2)
            softmax_corrections(B - 1)
            for j in range(J // 2 + 1):
                exp_half(B - 1, 1, j)
            for j in range(J // 2):
                scaled_g_hi(B - 1, 0, j)
            for j in range(J // 2 + 1, J):
                exp_half(B - 1, 1, j)
            for j in range(J // 2, J):
                scaled_g_hi(B - 1, 0, j)
            main(None, B - 1)
            copy_y(B - 1, K - 1)

            def y2_hi(t, n):
                act.wait_ge(y2_in[n], t * 16 + 16)
                wait(act, wy2_mm, before(t, n) * CH - CH)
                s = 2 * turn(t, n)
                nc.scalar.activation(ring_hi[:, s:s + 2, :], y2[n], ACT.Identity).then_inc(y2_hi_made, 1)

            def scale_shift(t, n):
                if isinstance(t, int) and (t, n) == FIRST[0]:
                    act.wait_ge(affine_ready, 1)
                for c in range(CH):
                    pair = pairs[CH * turn(t, n) + c]
                    act.wait_ge(wy2_mm, before(t, n) * CH + (c + 1))
                    nc.scalar.activation(pair, pair, ACT.Identity, bias=bn_shift[:, c:c + 1],
                                         scale=bn_scale[:, c:c + 1]).then_inc(wy2_scaled, 1)

            def store(t, n):
                act.wait_ge(x_added, before(t, n) * CH + CH)
                b, cols = in_dram(t, n)
                for c in range(CH):
                    act.dma_start(out_v[b, :, c, cols].rearrange("p (h n) -> p h n", h=2),
                                  x2[n][c]).then_inc(out_done[n], 16)

            def second(former, pieces, following):
                for piece, nxt in zip(pieces, pieces[1:] + [following]):
                    if nxt:
                        y2_hi(*nxt)
                    if former:
                        store(*former)
                    scale_shift(*piece)
                    former = piece

            y2_hi(*FIRST[0])
            act.wait_ge(bn_img_done, 2 * B + 1)
            nc.scalar.activation(bn_tmp[:, 1, :], bn_tmp[:, 0, :], ACT.Sqrt).then_inc(sqrt_done, 1)
            second(None, FIRST, (1, 0))
            with act.Fori(1, ROUNDS) as t:
                second((t - 1, NBUF - 1), round_of(t), (t + 1, 0))
            second((ROUNDS - 1, NBUF - 1), LAST, None)
            store(*LAST[-1])

        @block.vector
        def _(dve):
            def low_of_weights():
                dve.wait_ge(w_split_hi, 1)
                nc.vector.tensor_tensor(w_lo[:, :, :, :], w_stage, f32(w_hi[:, :, :, :]),
                                        ALU.subtract).then_inc(w_split_lo, 1)

            def low_of_W():
                dve.wait_ge(w_split_hi, 2)
                nc.vector.tensor_tensor(W_lo[:, :], W_stage, f32(W_hi[:, :]), ALU.subtract).then_inc(w_split_lo, 1)
                nc.vector.memset(tokens[:, :, :], float(N)).then_inc(w_split_lo, 1)
                dve.wait_ge(w_split_lo, 3)

            def proj_x_hi(b, k):
                wait_x_in(dve, b, k)
                wait_proj_x_free(dve, b, k)
                hi, lo = proj_x(k)
                nc.vector.tensor_copy(hi, x_raw[:, BUF[k], :, :]).then_inc(xhi_proj, 1)
                if k in DVE_X:
                    wait(dve, xhi_proj, blk(b, k) + 1)
                    nc.vector.tensor_tensor(lo[:, 1, :], x_raw[:, BUF[k], 1, :], f32(hi[:, 1, :]),
                                            ALU.subtract).then_inc(xlo_proj_dve, 1)

            window = "p (h a w t) -> p h w a t"
            sizes = dict(a=2, w=ROW // 2, t=2)

            def pool_phi(b, k):
                if k >= 2:
                    wait(dve, phi_lo_made, blk(b, k - 1))
                wait(dve, phi_mm, blk(b, k) + 1)
                nc.vector.tensor_reduce(phi_raw[:, k % 2, :].rearrange("p (h w) -> p h w", w=ROW // 2),
                                        f_ps[:, 2 * (k % 2), :].rearrange(window, **sizes), AX.XY,
                                        ALU.max).then_inc(phi_pooled, 1)

            def pool_g(b, k):
                if k >= 2:
                    wait(dve, gT_mm, blk(b, k - 1))
                wait(dve, g_mm, blk(b, k) + 1)
                nc.vector.tensor_reduce(g_raw[:, k % 2, :].rearrange("p (h w) -> p h w", w=ROW // 2),
                                        f_ps[:, 2 * (k % 2) + 1, :].rearrange(window, **sizes), AX.XY,
                                        ALU.max).then_inc(g_pooled, 1)

            def phi_low(b, k):
                wait(dve, phi_hi_made, blk(b, k) + 1)
                wait(dve, phi_pooled, blk(b, k) + 1)
                cols = slice(k * P, (k + 1) * P)
                nc.vector.scalar_tensor_tensor(phi_lo[:, cols], phi_raw[:, k % 2, :], bias[:, 1:2],
                                               f32(phi_hi[:, cols]), ALU.add, ALU.subtract).then_inc(phi_lo_made, 1)

            def copy_gT(b, k):
                wait(dve, gT_mm, blk(b, k) + 1)
                nc.vector.tensor_tensor(gT[:, par(b), k, :], y_ps[:, 0:P], g_bias[:, :],
                                        ALU.add).then_inc(gT_copied, 1)

            def theta_lo(b, k):
                wait(dve, th_hi_made, blk(b, k) + 1)
                hi, lo = theta_tile(b, k)
                nc.vector.scalar_tensor_tensor(lo, t_ps, bias[:, 0:1], f32(hi),
                                               ALU.add, ALU.subtract).then_inc(th_lo_made, 1)

            def store_f(b, k, j, v):
                wait(dve, f_mm, tile(b, k, j) + 1)
                if v is not None:
                    wait_p_lo(dve, v, k, j)
                if j == 0:
                    wait(dve, max_made, 2 * b + k // HK)
                nc.vector.tensor_scalar(exp_tile(k, j), f_ps[:, j % 4, :], 1.0, None, ALU.mult, ALU.max,
                                        accum_out=block_max[:, j, k:k + 1]).then_inc(f_stored, 1)

            def exp_lo(v, k, j):
                if j in POOL_J:
                    return
                wait(dve, p_hi_made, tile(v, k, j) + 1)
                nc.vector.tensor_tensor(ring_lo[:, slot(j), :], exp_tile(k, j), f32(ring_hi[:, slot(j), :]),
                                        ALU.subtract).then_inc(p_lo_dve, 1)

            def half_max(b, h):
                wait(dve, f_stored, tile(b, (h + 1) * HK, 0))
                wait(dve, exp_done, b * (2 * J))
                wait(dve, shift_made, b * 2)
                nc.vector.tensor_reduce(neg_max[:, h, :], block_max[:, :, h * HK:(h + 1) * HK], AX.X, ALU.max,
                                        negate=True).then_inc(max_made, 1)

            def max_shift(b):
                wait(dve, max_made, 2 * b + 2)
                wait(dve, corr_made, b)
                nc.vector.tensor_tensor(neg_all[:, :], neg_max[:, 0, :], neg_max[:, 1, :],
                                        ALU.min).then_inc(shift_made, 1)
                wait(dve, shift_made, 2 * b + 1)
                for h in range(2):
                    last = nc.vector.tensor_tensor(shift_h[:, h, :], neg_all[:, :], neg_max[:, h, :], ALU.subtract)
                last.then_inc(shift_made, 1)

            def softmax_factors(b, part=None):
                js = slice(0, J) if part is None else slice(part * (J // 2), (part + 1) * (J // 2))
                wait(dve, exp_done, b * (2 * J) + (J + js.stop))
                wait(dve, corr_made, b + 1)
                wait(dve, gn_lo_made, b * (2 * J))
                links = 3 * b + 3 * (part or 0)
                nc.vector.tensor_tensor(part_sum[:, :, js], half_sum[:, :, js], corr[:, :, js],
                                        ALU.mult).then_inc(chain, 1)
                wait(dve, chain, links + 1)
                nc.vector.tensor_tensor(total[:, js], part_sum[:, 0, js], part_sum[:, 1, js],
                                        ALU.add).then_inc(chain, 1)
                wait(dve, chain, links + 2)
                nc.vector.reciprocal(inv_total[:, js], total[:, js]).then_inc(chain, 1)
                wait(dve, chain, links + 3)
                for h in range(2):
                    last = nc.vector.tensor_tensor(factor[:, h, js], corr[:, h, js], inv_total[:, js], ALU.mult)
                last.then_inc(factor_made, 1)

            def scaled_g_lo(v, h, j):
                if j == 0 or (last_image(v) and j == J // 2):
                    wait(dve, factor_made, v + (1 if j == 0 else 2))
                wait(dve, gn_hi_made, v * (2 * J) + (h * J + j + 1))
                nc.vector.scalar_tensor_tensor(gn_lo[:, j, :], gT[:, par(v), j, :], factor[:, h, j:j + 1],
                                               f32(gn_hi[:, j, :]), ALU.mult, ALU.subtract).then_inc(gn_lo_made, 1)

            def y_low(v, k):
                wait(dve, y_hi_made, blk(v, k) + 1)
                nc.vector.tensor_tensor(y_lo[:, :], y32[:, :], f32(y_hi[:, :]),
                                        ALU.subtract).then_inc(y_lo_made, 1)

            def block_stats(v, k):
                wait(dve, wy_mm, blk(v, k) + 1)
                if k == 0:
                    wait(dve, bn_img_done, 2 * v)
                for c in range(CH):
                    last = nc.vector.bn_stats(bn_blk[:, c, k, :], wy_ps[:, c, :])
                last.then_inc(bn_done, 1)

            def image_stats(v):
                wait(dve, bn_done, blk(v, K))
                nc.vector.tensor_scalar(bn_all[:, :, bass.ds(v, 1), 0], tokens[:, :, :], 1.0, None, ALU.mult)
                for c in range(CH):
                    last = nc.vector.bn_aggr(bn_img[:, c, :], bn_blk[:, c, :, :])
                last.then_inc(bn_img_done, 1)
                wait(dve, bn_img_done, 2 * v + 1)
                nc.vector.tensor_copy(bn_all[:, :, bass.ds(v, 1), 1], bn_img[:, :, 0:1])
                nc.vector.tensor_scalar(bn_all[:, :, bass.ds(v, 1), 2], bn_img[:, :, 1:2], float(N), None,
                                        ALU.mult).then_inc(bn_img_done, 1)

            def projections(b, e=None, v=None):
                if first_image(b):
                    proj_x_hi(b, 0)
                if e is not None:
                    half_max(e, 1)
                    max_shift(e)
                if v is not None:
                    y_low(v, K - 1)
                    block_stats(v, K - 2)
                proj_x_hi(b, 1)
                for k in range(K):
                    if k < K - 2:
                        proj_x_hi(b, k + 2)
                    if k >= 1:
                        phi_low(b, k - 1)
                    pool_phi(b, k)
                    if e is not None and k == K - 2:
                        softmax_factors(e)
                    if e is not None and k == K - 1:
                        scaled_g_lo(e, 0, 0)
                        scaled_g_lo(e, 0, 1)
                    pool_g(b, k)
                    if k >= 1:
                        copy_gT(b, k - 1)
                    if k == 0:
                        theta_lo(b, 0)
                    if v is not None:
                        if k == 4:
                            block_stats(v, K - 1)
                        if k == 5:
                            image_stats(v)
                phi_low(b, K - 1)
                copy_gT(b, K - 1)
                if e is not None:
                    exp_lo(e, 0, 0)
                    scaled_g_lo(e, 0, 2)
                    scaled_g_lo(e, 0, 3)

            def main(b=None, v=None):
                for k in range(K):
                    for j in range(J):
                        if v is not None:
                            k2, j2 = (k, j + 1) if j + 1 < J else (k + 1, 0)
                            if k2 == k and not (k == 0 and last_image(v)):
                                exp_lo(v, k2, j2)
                        if v is None and k < K - 1 and j == (6 if k else 0):
                            theta_lo(b, k + 1)
                        if k == K - 1 and j == (4 if v is None else J - 1) and b is not None and not last_image(b):
                            proj_x_hi(b + 1, 0)
                        if v is not None and b is not None and k == 0 and j == J - 1:
                            theta_lo(b, 1)
                        if b is not None:
                            store_f(b, k, j, v)
                        if v is not None and j == J - 1:
                            if b is not None and 0 < k < K - 1:
                                theta_lo(b, k + 1)
                            if k < K - 1:
                                exp_lo(v, k + 1, 0)
                        if v is not None:
                            if k == 0 and j < 4 and not last_image(v):
                                scaled_g_lo(v, 0, j + 4)
                            if j == (3 if last_image(v) else 1) and k >= 1:
                                y_low(v, k - 1)
                            if j == (1 if last_image(v) else 3) and k >= 2:
                                block_stats(v, k - 2)
                            if k == HK - 1 and j >= 2:
                                scaled_g_lo(v, 1, j - 2)
                    if v is not None and k == HK - 1:
                        scaled_g_lo(v, 1, J - 2)
                        scaled_g_lo(v, 1, J - 1)
                    if b is not None and k == HK - 1:
                        half_max(b, 0)

            def y2_lo(t, n):
                dve.wait_ge(y2_hi_made, before(t, n) + 1)
                s = 2 * turn(t, n)
                nc.vector.tensor_tensor(ring_lo[:, s:s + 2, :], y2[n], f32(ring_hi[:, s:s + 2, :]),
                                        ALU.subtract).then_inc(y2_lo_made, 1)

            low_of_weights()
            projections(0)
            low_of_W()
            main(0)
            projections(1, 0)
            main(1, 0)
            projections(2, 1, 0)
            with dve.Fori(2, B - 1) as b:
                main(b, b - 1)
                projections(b + 1, b, b - 1)
            main(B - 1, B - 2)
            half_max(B - 1, 1)
            max_shift(B - 1)
            y_low(B - 2, K - 1)
            block_stats(B - 2, K - 2)
            block_stats(B - 2, K - 1)
            image_stats(B - 2)
            dve.wait_ge(exp_done, (B - 1) * (2 * J) + J)
            for part in range(2):
                js = range(part * (J // 2), (part + 1) * (J // 2))
                for j in js:
                    dve.wait_ge(y_mm, tile(B - 1, 0, j) - (3 if part else j))
                    nc.vector.tensor_copy(ring_hi[:, slot(j), :], exp_tile(0, j)).then_inc(p_hi_made, 1)
                for j in js:
                    exp_lo(B - 1, 0, j)
                softmax_factors(B - 1, part)
                for j in js:
                    scaled_g_lo(B - 1, 0, j)
            main(None, B - 1)
            block_stats(B - 1, K - 2)
            y_low(B - 1, K - 1)
            y2_lo(*FIRST[0])
            block_stats(B - 1, K - 1)
            image_stats(B - 1)

            count = [0]

            def link(instruction):
                count[0] += 1
                instruction.then_inc(chain, 1)
                dve.wait_ge(chain, 3 * (B + 1) + count[0])

            dve.wait_ge(bn_img_done, 2 * B)
            for c in range(CH):
                link(nc.vector.bn_aggr(bn_tot[:, c, :], bn_all[:, c, :, :]))
            var_eps, root, guess, mean_all, tmp, tmp2, centred = (bn_tmp[:, i, :] for i in range(7))
            nc.vector.tensor_scalar(var_eps, bn_tot[:, :, 1], BN_EPS, None, ALU.add).then_inc(bn_img_done, 1)
            link(nc.vector.tensor_tensor(mean_all, bn_tot[:, :, 0], chans[:, :, 0], ALU.add))
            link(nc.vector.tensor_tensor(centred, chans[:, :, 0], mean_all, ALU.subtract))
            dve.wait_ge(sqrt_done, 1)
            link(nc.vector.reciprocal(guess, root))
            link(nc.vector.tensor_tensor(tmp, guess, guess, ALU.mult))
            link(nc.vector.tensor_tensor(tmp2, tmp, var_eps, ALU.mult))
            link(nc.vector.tensor_scalar(tmp, tmp2, -0.5, 1.5, ALU.mult, ALU.add))
            link(nc.vector.tensor_tensor(tmp2, guess, tmp, ALU.mult))
            link(nc.vector.tensor_tensor(bn_scale[:, :], tmp2, chans[:, :, 1], ALU.mult))
            link(nc.vector.tensor_tensor(tmp2, centred, bn_scale[:, :], ALU.mult))
            nc.vector.tensor_tensor(bn_shift[:, :], tmp2, chans[:, :, 2], ALU.add).then_inc(affine_ready, 1)

            def add_x(t, n):
                dve.wait_ge(x2_in[n], t * (16 * CH) + 16 * CH)
                for c in range(CH):
                    dve.wait_ge(wy2_scaled, before(t, n) * CH + (c + 1))
                    nc.vector.tensor_tensor(x2[n][c], pairs[CH * turn(t, n) + c], x2[n][c],
                                            ALU.add).then_inc(x_added, 1)

            def second(pieces, following):
                for piece, nxt in zip(pieces, pieces[1:] + [following]):
                    if nxt:
                        y2_lo(*nxt)
                    add_x(*piece)

            second(FIRST, (1, 0))
            with dve.Fori(1, ROUNDS) as t:
                second(round_of(t), (t + 1, 0))
            second(LAST, None)

        @block.gpsimd
        def _(pool):
            def proj_x_lo(b, k):
                hi, lo = proj_x(k)
                wait(pool, xhi_proj, blk(b, k) + 1)
                for c in range(1 if k in DVE_X else CH):
                    last = nc.gpsimd.tensor_tensor(lo[:, c, :], x_raw[:, BUF[k], c, :], f32(hi[:, c, :]), ALU.subtract)
                last.then_inc(xlo_proj, 1)

            def theta_x_lo(b, k, c):
                wait(pool, xhi_theta, b * (2 * (K - 2)) + (2 * (k - 2) + c + 1))
                nc.gpsimd.tensor_tensor(xm_lo[:, :], x_raw[:, BUF[K + k - 2], c, :], f32(xm_hi[:, :]),
                                        ALU.subtract).then_inc(xlo_theta, 1)

            def projections(b):
                for k in range(K):
                    proj_x_lo(b, k)

            def main(b=None, v=None):
                for k in range(K):
                    for n, j in enumerate(POOL_J):
                        if v is not None:
                            wait(pool, p_hi_made, tile(v, k, j) + 1)
                            nc.gpsimd.tensor_tensor(ring_lo[:, slot(j), :], exp_tile(k, j),
                                                    f32(ring_hi[:, slot(j), :]),
                                                    ALU.subtract).then_inc(p_lo_pool, 1)
                        if b is not None and 1 <= k < K - 1:
                            if n == 0:
                                theta_x_lo(b, k + 1, 0)
                            if n == 2:
                                theta_x_lo(b, k + 1, 1)

            projections(0)
            main(0)
            projections(1)
            main(1, 0)
            projections(2)
            with pool.Fori(2, B - 1) as b:
                main(b, b - 1)
                projections(b + 1)
            main(B - 1, B - 2)
            main(None, B - 1)


def kernel(**inputs):
    import numpy as np
    import concourse.bacc as bacc
    from concourse import mybir as mb
    from concourse.bass_utils import run_bass_kernel_spmd as run

    def arr(name):
        return np.asarray(inputs[name])

    x = np.ascontiguousarray(arr("x"))
    B, C, H, W = x.shape
    arrays = {
        "x_dram": x.reshape(B, C, H * W),
        "wT_dram": np.ascontiguousarray(np.stack([arr(f"L0_conv_{n}_w").T for n in ("theta", "phi", "g")], axis=1)),
        "bias_dram": np.ascontiguousarray(np.stack([arr(f"L0_conv_{n}_b") for n in ("theta", "phi")], axis=1)),
        "g_bias_dram": np.ascontiguousarray(np.broadcast_to(arr("L0_conv_g_b"), (128, arr("L0_conv_g_b").size))),
        "WT_dram": np.ascontiguousarray(arr("L0_conv_W_w").T),
        "chan_dram": np.ascontiguousarray(
            np.stack([arr(f"L0_conv_{n}") for n in ("W_b", "bn_gamma", "bn_beta")], axis=1)),
        "ident_dram": np.eye(128, dtype=np.float32),
    }
    IC = arrays["WT_dram"].shape[0]
    nc = bacc.Bacc("TRN2", target_bir_lowering=False, num_devices=1)
    args = [nc.dram_tensor(n, a.shape, mb.dt.from_np(a.dtype), kind="ExternalInput").ap() for n, a in arrays.items()]
    out = nc.dram_tensor("out_dram", (B, C, H * W), mb.dt.float32, kind="ExternalOutput").ap()
    y = nc.dram_tensor("y_dram", (B, IC, H * W), mb.dt.float32).ap()
    nonlocal_block_kernel(nc, *args, out, y)
    r = run(nc, [arrays], core_ids=[0])
    return r.results[0]["out_dram"].reshape(B, C, H, W)
```
